# Optimizing a Trainium2 kernel written in Bass

```python
import numpy as np
import jax
import jax.numpy as jnp

def _softmax(x, axis=-1):
    return jax.nn.softmax(x, axis=axis)

def _gelu(x):
    return jax.nn.gelu(x, approximate=True)

def _silu(x):
    return jax.nn.silu(x)

def _sigmoid(x):
    return jax.nn.sigmoid(x)

def _layernorm(x, axis=-1, eps=1e-05):
    m = jnp.mean(x, axis=axis, keepdims=True)
    v = jnp.var(x, axis=axis, keepdims=True)
    return (x - m) / jnp.sqrt(v + eps)

def _scatter_add(tgt, idx, src, axis=0):
    return tgt.at[idx].add(src)

def _segment_sum(src, seg, n):
    return jax.ops.segment_sum(src, seg, n)
kernel_name = 'mk_decoder_postln_d1_seqx_r4_c12c78'

def setup_inputs(seed: int=0):
    np.random.seed(seed)
    _w = jnp.asarray

    def _rec_inputs():
        import jax
        import jax.numpy as jnp
        _rk = jax.random.key(seed)
        x = 7.22e-05 + 1 * jax.random.normal(jax.random.fold_in(_rk, 1), (16, 112, 256), jnp.float32)
        _lenS = 112 - jax.random.randint(jax.random.fold_in(_rk, 7), (16,), 0, max(1, 112 // 4) + 1, jnp.int32)
        _lenS2 = 375 - jax.random.randint(jax.random.fold_in(_rk, 8), (16,), 0, max(1, 375 // 4) + 1, jnp.int32)
        _ctx_768P = jax.random.normal(jax.random.fold_in(_rk, 11), (16, 16, 192), jnp.float32)
        _ctx_768c = jax.random.dirichlet(jax.random.fold_in(_rk, 511), 0.3 * jnp.ones((16,), jnp.float32), (16, 375))
        _ctx_768t = jnp.einsum('bsk,bkd->bsd', _ctx_768c, _ctx_768P)
        _ctx_768t = _ctx_768t * jax.lax.rsqrt(jnp.mean(jnp.square(_ctx_768t)) + 1e-12) * 0.953939
        ctx_768 = -0.000191848 + 0.999787 * (_ctx_768t + 0.3 * jax.random.normal(jax.random.fold_in(_rk, 611), (16, 375, 192), jnp.float32))
        return (x, ctx_768)
    x, ctx_768 = _rec_inputs()

    def _L0_attn_setup():
        import jax, jax.numpy as jnp
        import numpy as np
        DIM_Q = 256
        DIM_K = 256
        DIM_V = 256
        OUT_DIM = 256
        B, N = (4, 512)

        def _layer_norm(h, gamma, beta, eps=1e-05):
            mu = jnp.mean(h, axis=-1, keepdims=True)
            var = jnp.mean(jnp.square(h - mu), axis=-1, keepdims=True)
            return (h - mu) * jax.lax.rsqrt(var + eps) * gamma + beta
        key = jax.random.key(seed)
        ks = jax.random.split(key, 8)
        s_in = 1.0 / np.sqrt(DIM_Q)
        s_v = 1.0 / np.sqrt(DIM_V)
        return {'x': jax.random.normal(ks[0], (B, N, DIM_Q), dtype=jnp.float32), 'Wq': jax.random.normal(ks[1], (DIM_Q, DIM_K), dtype=jnp.float32) * s_in, 'Wk': jax.random.normal(ks[2], (DIM_Q, DIM_K), dtype=jnp.float32) * s_in, 'Wv': jax.random.normal(ks[3], (DIM_Q, DIM_V), dtype=jnp.float32) * s_in, 'Wfc': jax.random.normal(ks[4], (DIM_V, OUT_DIM), dtype=jnp.float32) * s_v, 'bfc': jax.random.normal(ks[5], (OUT_DIM,), dtype=jnp.float32) * 0.02, 'gamma': jnp.ones((DIM_V,), dtype=jnp.float32), 'beta': jnp.zeros((DIM_V,), dtype=jnp.float32)}
    _L0_attn_all = _L0_attn_setup()
    _L0_attn_in = {k: v for k, v in _L0_attn_all.items() if k in ('Wq', 'Wk', 'Wv', 'Wfc', 'bfc', 'gamma', 'beta')}
    del _L0_attn_all

    def _L0_xattn_setup():
        import jax, jax.numpy as jnp
        import numpy as np
        NUM_HEADS = 16
        CLAMP = 10000.0
        key = jax.random.key(seed)
        ks = jax.random.split(key, 8)
        B, Nq, Nkv, Cq, Ckv = (4, 512, 512, 256, 192)
        s_q = 1.0 / np.sqrt(Cq)
        s_kv = 1.0 / np.sqrt(Ckv)
        return {'query': jax.random.normal(ks[0], (B, Nq, Cq), jnp.float32), 'key_value': jax.random.normal(ks[1], (B, Nkv, Ckv), jnp.float32), 'Wq': jax.random.normal(ks[2], (Cq, Cq), jnp.float32) * s_q, 'bq': jnp.zeros((Cq,), jnp.float32), 'Wk': jax.random.normal(ks[3], (Ckv, Cq), jnp.float32) * s_kv, 'bk': jnp.zeros((Cq,), jnp.float32), 'Wv': jax.random.normal(ks[4], (Ckv, Cq), jnp.float32) * s_kv, 'bv': jnp.zeros((Cq,), jnp.float32), 'Wo': jax.random.normal(ks[5], (Cq, Cq), jnp.float32) * s_q, 'bo': jnp.zeros((Cq,), jnp.float32)}
    _L0_xattn_all = _L0_xattn_setup()
    _L0_xattn_in = {k: v for k, v in _L0_xattn_all.items() if k in ('Wq', 'bq', 'Wk', 'bk', 'Wv', 'bv', 'Wo', 'bo')}
    del _L0_xattn_all

    def _L0_ffn_setup():
        import jax, jax.numpy as jnp
        import numpy as np
        BLOCK = 16
        _GRID = jnp.array([0.0, 0.5, 1.0, 1.5, 2.0, 3.0, 4.0, 6.0], dtype=jnp.float32)
        _MID = jnp.array([0.25, 0.75, 1.25, 1.75, 2.5, 3.5, 5.0], dtype=jnp.float32)

        def fp4_quant_dequant(x):
            shape = x.shape
            xb = x.reshape(shape[:-1] + (shape[-1] // BLOCK, BLOCK))
            scale = jnp.max(jnp.abs(xb), axis=-1, keepdims=True) / 6.0
            scale = jnp.maximum(scale, jnp.float32(1e-12))
            xn = xb / scale
            idx = jnp.searchsorted(_MID, jnp.abs(xn))
            q = _GRID[idx] * jnp.sign(xn) * scale
            return q.reshape(shape)

        def fp4_linear(x, w):
            xq = fp4_quant_dequant(x)
            wq = fp4_quant_dequant(w)
            return jnp.einsum('bsk,nk->bsn', xq, wq)
        key = jax.random.key(seed)
        k1, k2, k3, k4 = jax.random.split(key, 4)
        H, I = (256, 704)
        x = jax.random.normal(k1, (4, 1024, H), dtype=jnp.float32)
        w_gate = jax.random.normal(k2, (I, H), dtype=jnp.float32) * 0.02
        w_up = jax.random.normal(k3, (I, H), dtype=jnp.float32) * 0.02
        w_down = jax.random.normal(k4, (H, I), dtype=jnp.float32) * 0.02
        return {'x': x, 'w_gate': w_gate, 'w_up': w_up, 'w_down': w_down}
    _L0_ffn_all = _L0_ffn_setup()
    _L0_ffn_in = {k: v for k, v in _L0_ffn_all.items() if k in ('w_gate', 'w_up', 'w_down')}
    del _L0_ffn_all
    return {'x': x, 'ctx_768': ctx_768, 'L0_attn_Wq': _L0_attn_in['Wq'], 'L0_attn_Wk': _L0_attn_in['Wk'], 'L0_attn_Wv': _L0_attn_in['Wv'], 'L0_attn_Wfc': _L0_attn_in['Wfc'], 'L0_attn_bfc': _L0_attn_in['bfc'], 'L0_attn_gamma': _L0_attn_in['gamma'], 'L0_attn_beta': _L0_attn_in['beta'], 'L0_xattn_Wq': _L0_xattn_in['Wq'], 'L0_xattn_bq': _L0_xattn_in['bq'], 'L0_xattn_Wk': _L0_xattn_in['Wk'], 'L0_xattn_bk': _L0_xattn_in['bk'], 'L0_xattn_Wv': _L0_xattn_in['Wv'], 'L0_xattn_bv': _L0_xattn_in['bv'], 'L0_xattn_Wo': _L0_xattn_in['Wo'], 'L0_xattn_bo': _L0_xattn_in['bo'], 'L0_ffn_w_gate': _L0_ffn_in['w_gate'], 'L0_ffn_w_up': _L0_ffn_in['w_up'], 'L0_ffn_w_down': _L0_ffn_in['w_down']}

def reference(x, ctx_768, L0_attn_Wq, L0_attn_Wk, L0_attn_Wv, L0_attn_Wfc, L0_attn_bfc, L0_attn_gamma, L0_attn_beta, L0_xattn_Wq, L0_xattn_bq, L0_xattn_Wk, L0_xattn_bk, L0_xattn_Wv, L0_xattn_bv, L0_xattn_Wo, L0_xattn_bo, L0_ffn_w_gate, L0_ffn_w_up, L0_ffn_w_down):
    import jax
    import jax.numpy as jnp

    def _L0_attn_ref(x, Wq, Wk, Wv, Wfc, bfc, gamma, beta):
        import jax, jax.numpy as jnp
        import numpy as np
        DIM_Q = 256
        DIM_K = 256
        DIM_V = 256
        OUT_DIM = 256
        B, N = (4, 512)

        def _layer_norm(h, gamma, beta, eps=1e-05):
            mu = jnp.mean(h, axis=-1, keepdims=True)
            var = jnp.mean(jnp.square(h - mu), axis=-1, keepdims=True)
            return (h - mu) * jax.lax.rsqrt(var + eps) * gamma + beta
        q = jnp.einsum('bnd,dk->bnk', x, Wq)
        k = jnp.einsum('bnd,dk->bnk', x, Wk)
        v = jnp.einsum('bnd,dv->bnv', x, Wv)
        scale = 1.0 / np.sqrt(DIM_K)
        scores = jnp.einsum('bnk,bmk->bnm', q, k) * scale
        n = x.shape[1]
        causal = jnp.tril(jnp.ones((n, n), dtype=bool))
        scores = jnp.where(causal, scores, -jnp.inf)
        att = jax.nn.softmax(scores, axis=-1)
        out = jnp.einsum('bnm,bmv->bnv', att, v)
        out = _layer_norm(out + v, gamma, beta)
        return jnp.einsum('bnv,vo->bno', out, Wfc) + bfc

    def _L0_xattn_ref(query, key_value, Wq, bq, Wk, bk, Wv, bv, Wo, bo):
        import jax, jax.numpy as jnp
        import numpy as np
        NUM_HEADS = 16
        CLAMP = 10000.0
        B, Nq, Cq = query.shape
        Nkv = key_value.shape[1]
        H = NUM_HEADS
        D = Cq // H
        scale = D ** (-0.5)
        q = (query @ Wq + bq).reshape(B, Nq, H, D).transpose(0, 2, 1, 3)
        k = (key_value @ Wk + bk).reshape(B, Nkv, H, D).transpose(0, 2, 1, 3)
        v = (key_value @ Wv + bv).reshape(B, Nkv, H, D).transpose(0, 2, 1, 3)
        attn = jnp.einsum('bhqd,bhkd->bhqk', q, k) * scale
        attn = jnp.clip(attn, -CLAMP, CLAMP)
        attn = jax.nn.softmax(attn, axis=-1)
        attn = jnp.where(jnp.any(jnp.isnan(attn)), jnp.asarray(1.0 / Nkv, attn.dtype), attn)
        x = jnp.einsum('bhqk,bhkd->bqhd', attn, v).reshape(B, Nq, Cq)
        return x @ Wo + bo

    def _L0_ffn_ref(x, w_gate, w_up, w_down):
        import jax, jax.numpy as jnp
        import numpy as np
        BLOCK = 16
        _GRID = jnp.array([0.0, 0.5, 1.0, 1.5, 2.0, 3.0, 4.0, 6.0], dtype=jnp.float32)
        _MID = jnp.array([0.25, 0.75, 1.25, 1.75, 2.5, 3.5, 5.0], dtype=jnp.float32)

        def fp4_quant_dequant(x):
            shape = x.shape
            xb = x.reshape(shape[:-1] + (shape[-1] // BLOCK, BLOCK))
            scale = jnp.max(jnp.abs(xb), axis=-1, keepdims=True) / 6.0
            scale = jnp.maximum(scale, jnp.float32(1e-12))
            xn = xb / scale
            idx = jnp.searchsorted(_MID, jnp.abs(xn))
            q = _GRID[idx] * jnp.sign(xn) * scale
            return q.reshape(shape)

        def fp4_linear(x, w):
            xq = fp4_quant_dequant(x)
            wq = fp4_quant_dequant(w)
            return jnp.einsum('bsk,nk->bsn', xq, wq)
        gate = fp4_linear(x, w_gate)
        y = fp4_linear(x, w_up)
        h = jax.nn.silu(gate) * y
        return fp4_linear(h, w_down)
    x = _layernorm(x + _L0_attn_ref(x, L0_attn_Wq, L0_attn_Wk, L0_attn_Wv, L0_attn_Wfc, L0_attn_bfc, L0_attn_gamma, L0_attn_beta), axis=-1)
    x = _layernorm(x + _L0_xattn_ref(x, ctx_768, L0_xattn_Wq, L0_xattn_bq, L0_xattn_Wk, L0_xattn_bk, L0_xattn_Wv, L0_xattn_bv, L0_xattn_Wo, L0_xattn_bo), axis=-1)
    x = _layernorm(x + _L0_ffn_ref(x, L0_ffn_w_gate, L0_ffn_w_up, L0_ffn_w_down), axis=-1)
    return x

_drawn_inputs = setup_inputs


def setup_inputs(seed=0):
    import zlib

    import numpy as np

    out = dict(_drawn_inputs(seed))
    spreads = {'L0_attn_gamma': (1.0, 0.2),
     'L0_attn_beta': (0.0, 0.1),
     'L0_xattn_bq': (0.0, 0.403),
     'L0_xattn_bk': (0.0, 0.8),
     'L0_xattn_bv': (0.0, 0.1),
     'L0_xattn_bo': (0.0, 0.1)}
    factors = {'L0_attn_bfc': 4.252}
    for name, (base, spread) in spreads.items():
        noise = np.random.default_rng([zlib.crc32(name.encode()), seed]).standard_normal(out[name].shape)
        drawn = base * np.exp(spread * noise) if base else spread * noise
        out[name] = jnp.asarray(drawn.astype(out[name].dtype))
    for name, factor in factors.items():
        out[name] = (out[name] * factor).astype(out[name].dtype)
    return out
```

```python
from contextlib import ExitStack

import concourse.bass as bass
from concourse import mybir

F32 = mybir.dt.float32
BF16 = mybir.dt.bfloat16
U32 = mybir.dt.uint32
I32 = mybir.dt.int32
ALU = mybir.AluOpType
ACT = mybir.ActivationFunctionType
X = mybir.AxisListType.X

B, N, D = 16, 112, 256
NK, DC = 375, 192
H, HD = 16, 16
FF, BLK = 704, 16
KC, KP = 3, 125
DK = D // 128
CK = DC // 2
WP, WJ = 88, 8
FT = [(c * 128, min(128, FF - c * 128)) for c in range((FF + 127) // 128)]
TERMS = [(0, 0), (1, 0), (2, 0), (0, 1), (1, 1), (0, 2)]
ROWS = 16 * len(TERMS)
SHIFT = 3
CLAMP = 10000.0
EPS = 1e-5
GROUPS = 4 * KC
HALF_UP = 4194304.0


class Steps:

    def __init__(self, base=0):
        self.base, self.n = base, 0

    def next(self):
        self.n += 1
        return self.base + self.n


def decoder_layer(nc, x, ctx_in, Wq, Wk, Wv, Wfc, bfc, gamma, beta, xWq, xbq, xWk, xbk, xWv, xbv, xWo, xbo,
                  w_gate, w_up, w_down, out):
    ctx = ExitStack()
    with ctx:
        def sb(name, shape, dt=F32):
            return ctx.enter_context(nc.sbuf_tensor(name, shape, dt))

        credited = []

        def sem(name, credit=0):
            made = ctx.enter_context(nc.semaphore(name))
            if credit:
                credited.append((made, credit))
            return made

        def two(name, credit=0):
            return [sem(f"{name}{p}", credit) for p in range(2)]

        ident = sb("ident", [128, 128])
        identb = sb("identb", [128, 128], BF16)
        x1 = sb("x1", [N, B, D])
        x1T = sb("x1T", [128, DK, B * N])
        heads = sb("heads", [N, B, D])
        vmeanT = sb("vmeanT", [128, DK, B])
        wsum = sb("wsum", [KP, B * GROUPS])
        wq, wk, wv, wfc = (sb(n, [128, DK, D]) for n in ("wq", "wk", "wv", "wfc"))
        xwq, xwo = (sb(n, [128, DK, D]) for n in ("xwq", "xwo"))
        xwk, xwv = (sb(n, [CK, 2, D]) for n in ("xwk", "xwv"))
        bfc_b, gamma_b, beta_b, bo_b = (sb(n, [N, D]) for n in ("bfc_b", "gamma_b", "beta_b", "bo_b"))
        bv_b = sb("bv_b", [KP, D])
        bqT, bkT, bvT = (sb(n, [128, DK]) for n in ("bqT", "bkT", "bvT"))
        wgT, wuT = sb("wgT", [128, DK, FF]), sb("wuT", [128, DK, FF])
        wdT = sb("wdT", [128, len(FT), D])
        causal = sb("causal", [N, N])
        mhalf = sb("mhalf", [128, 1])
        clampc = sb("clampc", [N, 1])

        arena = sb("arena", [128, 12288])
        place = [0]

        def carve(words):
            place[0] += words
            assert place[0] <= 12288
            return arena[:, place[0] - words:place[0]]

        raw_g = carve(WJ * D).rearrange("p (j k) -> p j k", k=D)
        raw_u = carve(WJ * D).rearrange("p (j k) -> p j k", k=D)
        raw_d = carve(2 * FF).rearrange("p (j k) -> p j k", k=FF)
        tmp = [carve(WJ * D) for _ in range(3)]
        place[0] = 0
        kst = [carve(H * NK // 2).bitcast(BF16).rearrange("p (h k) -> p h k", k=NK) for _ in range(2)]
        prob = [carve(KC * 4 * N).rearrange("p (c n) -> p c n", c=KC) for _ in range(4)]
        place[0] = 0
        hat = [carve(FF) for _ in range(2)]
        hq = [carve(FF) for _ in range(2)]
        ft = [[carve(FF) for _ in range(2)] for _ in range(2)]
        hqT = [carve(len(FT) * N).rearrange("p (c n) -> p c n", n=N) for _ in range(2)]
        att = [carve(D) for _ in range(2)]
        attT = [carve(DK * N).rearrange("p (k n) -> p k n", n=N) for _ in range(2)]
        x2 = [carve(D) for _ in range(2)]
        xq = [carve(D) for _ in range(2)]
        xqT = [carve(DK * N).rearrange("p (k n) -> p k n", n=N) for _ in range(2)]
        yo = [carve(D) for _ in range(2)]

        xs = [sb(f"xs{p}", [N, D]) for p in range(2)]
        xsT = [sb(f"xsT{p}", [128, DK, N]) for p in range(2)]
        qkT = [sb(f"qkT{p}", [128, 2 * DK, N]) for p in range(2)]
        vs = [sb(f"vs{p}", [N, D]) for p in range(2)]
        rest = [sb(f"rest{p}", [128, DK, NK + N]) for p in range(2)]
        lend = [r[0:N].rearrange("p k n -> p (k n)") for r in rest]
        sc, pr, prT = ([r[:, i * N:(i + 1) * N] for r in lend] for i in range(3))
        hs, x1s = ([r[:, 3 * N + i * D:3 * N + (i + 1) * D] for r in lend] for i in range(2))
        row = [sb(f"row{p}", [N, 4]) for p in range(2)]
        st6 = [sb(f"st6{p}", [N, 6]) for p in range(2)]
        mv = [sb(f"mv{p}", [N, 2]) for p in range(2)]
        rstd = [sb(f"rstd{p}", [N, 2]) for p in range(2)]

        cx = [sb(f"cx{p}", [KP, KC, DC]) for p in range(2)]
        cxsum = [sb(f"cxsum{p}", [CK, 2]) for p in range(2)]
        cxT = [sb(f"cxT{p}", [CK, 2, NK]) for p in range(2)]
        parts = [sb(f"parts{p}", [128, 3, DK, NK + N], BF16) for p in range(2)]
        qst = [sb(f"qst{p}", [ROWS + SHIFT, H, N], BF16) for p in range(2)]
        vx = [sb(f"vx{p}", [KP, KC, H, 32]) for p in range(2)]
        nmx = [sb(f"nmx{p}", [N, 3 * H]) for p in range(2)]
        mparts = [sb(f"mparts{p}", [N, 3, H], BF16) for p in range(2)]
        floor = [sb(f"floor{p}", [N, H]) for p in range(2)]
        mrow = [sb(f"mrow{p}", [3 * H, N], BF16) for p in range(2)]
        floorT = [sb(f"floorT{p}", [H, N]) for p in range(2)]
        floor_b = sb("floor_b", [KP, H * N])
        oT = qkT
        rden = [sb(f"rden{p}", [N, H]) for p in range(2)]
        scale = [sb(f"scale{p}", [128, 2 * 128]) for p in range(2)]
        flag = sb("flag", [128, B * GROUPS + 4])
        vmean = [sb(f"vmean{p}", [128, DK, 1]) for p in range(2)]
        nanmask = sb("nanmask", [128, 1], I32)
        ones = sb("ones", [KP, 128])

        kq_dram = nc.dram_tensor("kq_parts", [2, 3, H, HD, NK + N], BF16).ap()
        floor_dram = nc.dram_tensor("floor_rows", [2, H * N], F32).ap()

        bank = [ctx.enter_context(nc.psum_tensor(f"bank{i}", [128, 512], F32)) for i in range(8)]

        self_w, cross_w, ffn_w = sem("self_w"), sem("cross_w"), sem("ffn_w")
        consts = sem("consts")
        waits_met = sem("waits_met")
        dve_step = sem("dve_step")
        pool_step = sem("pool_step")
        w_quant, w_turned, w_kept = sem("w_quant"), sem("w_turned"), sem("w_kept")
        scaled = sem("scaled")
        stacks_one = sem("stacks_one")
        x_in, xT_ps, xT_ok = two("x_in"), sem("xT_ps"), sem("xT_ok")
        qk_ps, qk_ok, v_ps, v_ok = sem("qk_ps"), sem("qk_ok"), sem("v_ps"), sem("v_ok")
        s_ps, s_max, p_ok, pT_ps, pT_ok = sem("s_ps"), sem("s_max"), sem("p_ok"), sem("pT_ps"), sem("pT_ok")
        pv_ps, var_ok, rstd_ok = sem("pv_ps"), sem("var_ok"), sem("rstd_ok")
        h_ok, hT_ps, hT_ok, fc_ps = sem("h_ok"), sem("hT_ps"), sem("hT_ok"), sem("fc_ps")
        x1_ok, x1T_ps, x1T_ok = sem("x1_ok", 1), sem("x1T_ps"), sem("x1T_ok", 1)

        c_in, cT_ps, cT_ok = two("c_in"), sem("cT_ps", 1), sem("cT_ok")
        k_ps, k_hi, k_rest = sem("k_ps"), sem("k_hi"), sem("k_rest")
        vq_ps, vx_ok, q_hi, q_rest = sem("vq_ps"), sem("vx_ok"), sem("q_hi"), sem("q_rest", 1)
        vm_ps, vm_ok = sem("vm_ps"), sem("vm_ok", 1)
        split_ok, to_dram, stacked = sem("split_ok", 1), two("to_dram", 16), two("stacked", 16)
        sx_ps, sx_max = sem("sx_ps"), sem("sx_max", 2)
        neg_ok, mparts_ok, floor_ok = sem("neg_ok"), sem("mparts_ok"), sem("floor_ok")
        mT_ps, mT_ok = sem("mT_ps"), sem("mT_ok")
        mrow_in, floor_out, floor_in = two("mrow_in", 16), two("floor_out", 16), two("floor_in")
        st_ps, exp_ok, clip_ok = sem("st_ps"), sem("exp_ok", 2), sem("clip_ok", 1)
        prob_free = sem("prob_free", 4)
        oT_ok, o_ps, heads_ok = sem("oT_ok", 1), sem("o_ps", 1), sem("heads_ok", 1)

        nan_cnt, nan_ps, nan_ok = sem("nan_cnt"), sem("nan_ps"), sem("nan_ok")
        att_ok, aT_ps, aT_cp, aT_ok = sem("att_ok"), sem("aT_ps", 1), sem("aT_cp"), sem("aT_ok")
        wo_ps, xq_ok, xqT_ps, xqT_ok = sem("wo_ps"), sem("xq_ok"), sem("xqT_ps"), sem("xqT_ok")
        gate_ps, up_ps, silu_ok, hq_ok = sem("gate_ps"), sem("up_ps"), sem("silu_ok"), sem("hq_ok")
        hqT_ps, hqT_ok, dn_ps, y_ok = sem("hqT_ps"), sem("hqT_ok"), sem("dn_ps"), sem("y_ok", 1)
        y_out = two("y_out", 16)
        varf, rstdf = sem("varf"), sem("rstdf")

        block = ctx.enter_context(nc.Block())

        @block.sync
        def _(sp):
            def rows_of(w):
                return w.rearrange("(k p) n -> p k n", p=128)

            sp.dma_start(wq[:], rows_of(Wq)).then_inc(self_w, 16)
            sp.dma_start(wk[:], rows_of(Wk)).then_inc(self_w, 16)
            sp.dma_start(wv[:], rows_of(Wv)).then_inc(self_w, 16)
            sp.dma_start(wfc[:], rows_of(Wfc)).then_inc(self_w, 16)
            sp.dma_start(bfc_b[:], bfc.partition_broadcast(N)).then_inc(self_w, 16)
            sp.dma_start(gamma_b[:], gamma.partition_broadcast(N)).then_inc(self_w, 16)
            sp.dma_start(beta_b[:], beta.partition_broadcast(N)).then_inc(self_w, 16)
            sp.dma_start(raw_g[0:WP], w_gate.rearrange("(j p) k -> p j k", p=WP)).then_inc(ffn_w, 16)
            sp.dma_start(raw_u[0:WP], w_up.rearrange("(j p) k -> p j k", p=WP)).then_inc(ffn_w, 16)
            sp.dma_start(raw_d, w_down.rearrange("(j p) k -> p j k", p=128)).then_inc(ffn_w, 16)
            sp.dma_start(xwq[:], rows_of(xWq)).then_inc(cross_w, 16)
            sp.dma_start(xwo[:], rows_of(xWo)).then_inc(cross_w, 16)
            sp.dma_start(xwk[:], xWk.rearrange("(k p) n -> p k n", p=CK)).then_inc(cross_w, 16)
            sp.dma_start(xwv[:], xWv.rearrange("(k p) n -> p k n", p=CK)).then_inc(cross_w, 16)
            sp.dma_start(bo_b[:], xbo.partition_broadcast(N)).then_inc(cross_w, 16)
            sp.dma_start(bv_b[:], xbv.partition_broadcast(KP)).then_inc(cross_w, 16)
            sp.dma_start(bqT[:], xbq.rearrange("(k p) -> p k", p=128), allow_slow_non_contiguous=True).then_inc(cross_w, 16)
            sp.dma_start(bvT[:], xbv.rearrange("(k p) -> p k", p=128), allow_slow_non_contiguous=True).then_inc(cross_w, 16)
            sp.dma_start(bkT[:], xbk.rearrange("(k p) -> p k", p=128), allow_slow_non_contiguous=True).then_inc(cross_w, 16)
            with sp.Fori(0, B // 2) as it:
                for p in range(2):
                    sp.wait_ge(x1_ok, 2 * it + 1)
                    sp.sem_inc(waits_met, 1)
                    sp.dma_start(xs[p][:], x[it * 2 + p]).then_inc(x_in[p], 16)
            with sp.Fori(0, B // 2) as it:
                for p in range(2):
                    sp.wait_ge(cT_ps, 2 * it + 1)
                    sp.sem_inc(waits_met, 1)
                    sp.dma_start(cx[p][:], ctx_in[it * 2 + p].rearrange("(p c) d -> p c d", c=KC)).then_inc(c_in[p], 16)
                for p in range(2):
                    b = it * 2 + p
                    sp.wait_ge(split_ok, 4 * (b + 1) + 1)
                    sp.sem_inc(waits_met, 1)
                    sp.wait_ge(stacked[p], 16 * 12 * it + 16)
                    sp.sem_inc(waits_met, 1)
                    sp.dma_start(kq_dram[p].rearrange("t (m h) d k -> (h d) t m k", m=DK), parts[p][:]).then_inc(to_dram[p], 16)
                    sp.wait_ge(to_dram[p], 16 * (it + 1) + 16)
                    sp.sem_inc(waits_met, 1)
                    if p == 0:
                        sp.wait_ge(w_kept, 15)
                    sp.wait_ge(clip_ok, 4 * 2 * it + 1)
                    sp.sem_inc(waits_met, 1)
                    sp.wait_ge(heads_ok, 2 * it + 1)
                    sp.sem_inc(waits_met, 1)
                    for t, (pk, pq) in enumerate(TERMS):
                        sp.dma_start(kst[p][16 * t:16 * t + 16], kq_dram[p, pk, :, :, 0:NK].rearrange("h d k -> d h k")).then_inc(stacked[p], 16)
                        sp.dma_start(qst[p][16 * t:16 * t + 16], kq_dram[p, pq, :, :, NK:NK + N].rearrange("h d k -> d h k")).then_inc(stacked[p], 16)
                for p in range(2):
                    b = it * 2 + p
                    sp.wait_ge(mT_ok, b + 1)
                    sp.sem_inc(waits_met, 1)
                    for t in range(SHIFT):
                        sp.dma_start(qst[p][ROWS + t:ROWS + t + 1], mrow[p][16 * t:16 * t + 16, :]).then_inc(mrow_in[p], 16)
                    sp.dma_start(floor_dram[p].rearrange("(h q) -> h q", h=H), floorT[p][:]).then_inc(floor_out[p], 16)
                    sp.wait_ge(floor_out[p], 16 * (it + 1) + 16)
                    sp.sem_inc(waits_met, 1)
                    sp.wait_ge(clip_ok, 4 * b + 1)
                    sp.sem_inc(waits_met, 1)
                    sp.dma_start(floor_b[:], floor_dram[p].partition_broadcast(KP)).then_inc(floor_in[p], 16)
            with sp.Fori(0, B // 2) as it:
                for p in range(2):
                    b = it * 2 + p
                    sp.wait_ge(y_ok, b + 2)
                    sp.sem_inc(waits_met, 1)
                    sp.dma_start(out[b], yo[p][0:N]).then_inc(y_out[p], 16)
            for p in range(2):
                sp.wait_ge(y_out[p], 16 * B // 2 + 16)
            sp.sem_inc(waits_met, 1)

        @block.tensor
        def _(pe):
            def mm(o, l, r, start=True, stop=True):
                return nc.tensor.matmul(o, l, r, start=start, stop=stop)

            def turn(o, i, idt):
                return nc.tensor.transpose(o, i, idt)

            pe.wait_ge(consts, 1)
            n = 0
            for w, raw in enumerate((raw_g, raw_u)):
                pe.wait_ge(w_quant, w + 1)
                for k in range(DK):
                    for jh in range(2):
                        if n >= 8:
                            pe.wait_ge(w_kept, n - 7)
                        for j in range(4):
                            last = turn(bank[n % 8][:, j * WP:(j + 1) * WP], raw[0:WP, jh * 4 + j, k * 128:(k + 1) * 128], ident[0:WP, 0:WP])
                        last.then_inc(w_turned, 1)
                        n += 1
            pe.wait_ge(w_quant, 3)
            for c, (o, m) in enumerate(FT):
                if n >= 8:
                    pe.wait_ge(w_kept, n - 7)
                for j in range(2):
                    last = turn(bank[n % 8][0:m, j * 128:(j + 1) * 128], raw_d[:, j, o:o + m], ident[:, :])
                last.then_inc(w_turned, 1)
                n += 1
            pe.wait_ge(w_kept, 14)

            pe.wait_ge(self_w, 16 * 7)
            with pe.Fori(0, B // 2) as it:
                for p in range(2):
                    b = it * 2 + p
                    pe.wait_ge(x_in[p], 16 * (it + 1))
                    pe.wait_ge(x1T_ok, 2 * it + 1)
                    for k in range(DK):
                        last = turn(bank[4 * p][:, k * N:(k + 1) * N], xs[p][:, k * 128:(k + 1) * 128], ident[0:N, 0:N])
                    last.then_inc(xT_ps, 1)
                for p in range(2):
                    b = it * 2 + p
                    pe.wait_ge(xT_ok, b + 1)
                    for w, W in enumerate((wq, wk)):
                        for m in range(DK):
                            for k in range(DK):
                                last = mm(bank[4 * p + 1][:, (w * DK + m) * N:(w * DK + m + 1) * N], W[:, k, m * 128:(m + 1) * 128],
                                          xsT[p][:, k, :], start=(k == 0), stop=(k == DK - 1))
                    last.then_inc(qk_ps, 1)
                    for k in range(DK):
                        last = mm(bank[4 * p + 2][0:N, 0:D], xsT[p][:, k, :], wv[:, k, :], start=(k == 0), stop=(k == DK - 1))
                    last.then_inc(v_ps, 1)
                for p in range(2):
                    b = it * 2 + p
                    pe.wait_ge(qk_ok, b + 1)
                    for k in range(DK):
                        last = mm(bank[4 * p + 3][0:N, 0:N], qkT[p][:, k, :], qkT[p][:, DK + k, :], start=(k == 0), stop=(k == DK - 1))
                    last.then_inc(s_ps, 1)
                for p in range(2):
                    b = it * 2 + p
                    pe.wait_ge(p_ok, b + 1)
                    turn(bank[4 * p][0:N, 0:N], pr[p], ident[0:N, 0:N]).then_inc(pT_ps, 1)
                for p in range(2):
                    b = it * 2 + p
                    pe.wait_ge(pT_ok, b + 1)
                    pe.wait_ge(v_ok, b + 1)
                    mm(bank[4 * p + 1][0:N, 0:D], prT[p], vs[p][:]).then_inc(pv_ps, 1)
                for p in range(2):
                    b = it * 2 + p
                    pe.wait_ge(h_ok, b + 1)
                    for k in range(DK):
                        last = turn(bank[4 * p][:, k * N:(k + 1) * N], hs[p][:, k * 128:(k + 1) * 128], ident[0:N, 0:N])
                    last.then_inc(hT_ps, 1)
                for p in range(2):
                    b = it * 2 + p
                    pe.wait_ge(hT_ok, b + 1)
                    for k in range(DK):
                        last = mm(bank[4 * p + 1][0:N, 0:D], xsT[p][:, k, :], wfc[:, k, :], start=(k == 0), stop=(k == DK - 1))
                    last.then_inc(fc_ps, 1)
                for p in range(2):
                    b = it * 2 + p
                    pe.wait_ge(x1_ok, b + 2)
                    for k in range(DK):
                        last = turn(bank[4 * p][:, k * N:(k + 1) * N], x1s[p][:, k * 128:(k + 1) * 128], ident[0:N, 0:N])
                    last.then_inc(x1T_ps, 1)
            pe.wait_ge(x1T_ok, B + 1)

            pe.wait_ge(cross_w, 16 * 9)
            pe.wait_ge(scaled, 2)
            with pe.Fori(0, B // 2) as it:
                for p in range(2):
                    b = it * 2 + p
                    pe.wait_ge(c_in[p], 16 * (it + 1))
                    pe.wait_ge(vm_ok, b + 1)
                    pe.wait_ge(q_rest, b + 1)
                    for k in range(2):
                        for c in range(KC):
                            last = turn(bank[k][0:CK, c * KP:(c + 1) * KP], cx[p][:, c, k * CK:(k + 1) * CK], ident[0:KP, 0:KP])
                    last.then_inc(cT_ps, 1)
                    pe.wait_ge(cT_ok, b + 1)
                    for m in range(DK):
                        for k in range(2):
                            last = mm(bank[m][:, 0:NK], xwk[:, k, m * 128:(m + 1) * 128], cxT[p][:, k, :], start=(k == 0), stop=(k == 1))
                        last.then_inc(k_ps, 1)
                    pe.wait_ge(k_rest, DK * (b + 1))
                    for c in range(KC):
                        o = bank[c // 2][0:KP, (c % 2) * D:(c % 2 + 1) * D]
                        for k in range(2):
                            mm(o, cxT[p][:, k, c * KP:(c + 1) * KP], xwv[:, k, :], start=(k == 0), stop=(k == 1))
                    for m in range(DK):
                        for k in range(DK):
                            last = mm(bank[1][:, D + m * N:D + (m + 1) * N], xwq[:, k, m * 128:(m + 1) * 128],
                                      x1T[:, k, bass.ds(b * N, N)], start=(k == 0), stop=(k == DK - 1))
                    last.then_inc(vq_ps, 1)
                    pe.wait_ge(vx_ok, b + 1)
                    for m in range(DK):
                        for k in range(2):
                            last = mm(bank[0][:, m:m + 1], xwv[:, k, m * 128:(m + 1) * 128], cxsum[p][:, k:k + 1], start=(k == 0), stop=(k == 1))
                    last.then_inc(vm_ps, 1)
                for p in range(2):
                    b = it * 2 + p
                    pe.wait_ge(stacked[p], 16 * 12 * (it + 1) + 16)
                    for h in range(H):
                        pe.wait_ge(sx_max, b * H + h + 1)
                        mm(bank[2 + h % 2][0:N, 0:NK], qst[p][0:ROWS, h, :], kst[p][0:ROWS, h, :]).then_inc(sx_ps, 1)
                    pe.wait_ge(mparts_ok, b + 1)
                    pe.wait_ge(floor_ok, b + 1)
                    pe.wait_ge(heads_ok, 2 * it + 1)
                    pe.sem_inc(waits_met, 1)
                    turn(bank[7][0:3 * H, 0:N // 2].bitcast(BF16), mparts[p][:].rearrange("q t h -> q (t h)"), identb[0:N, 0:N])
                    turn(bank[7][0:H, 256:256 + N], floor[p][:], ident[0:N, 0:N]).then_inc(mT_ps, 1)
                    pe.wait_ge(mT_ok, b + 1)
                for p in range(2):
                    b = it * 2 + p

                    def weights_of(i):
                        for c in range(KC):
                            g = i * KC + c
                            pe.wait_ge(exp_ok, b * GROUPS + g + 1)
                            for j in range(4):
                                last = mm(bank[4 + g % 2][0:KP, j * N:(j + 1) * N], kst[p][0:ROWS + SHIFT, 4 * i + j, c * KP:(c + 1) * KP],
                                          qst[p][0:ROWS + SHIFT, 4 * i + j, :])
                            last.then_inc(st_ps, 1)

                    def values_of(i):
                        pe.wait_ge(clip_ok, 4 * b + i + 2)
                        for c in range(KC):
                            for j in range(4):
                                last = mm(bank[6][32 * j:32 * j + 32, i * N:(i + 1) * N], vx[p][:, c, 4 * i + j, :],
                                          prob[i][0:KP, c, j * N:(j + 1) * N], start=(c == 0), stop=(c == KC - 1))
                        last.then_inc(prob_free, 1)

                    pe.wait_ge(mrow_in[p], 16 * SHIFT * (it + 1) + 16)
                    pe.wait_ge(oT_ok, b + 1)
                    weights_of(0)
                    for i in range(1, 4):
                        weights_of(i)
                        values_of(i - 1)
                    values_of(3)
                    pe.wait_ge(oT_ok, b + 2)
                    pe.wait_ge(heads_ok, b + 1)
                    for i in range(4):
                        last = turn(bank[7][0:N, i * 128:(i + 1) * 128], oT[p][:, i, :], ident[:, :])
                    last.then_inc(o_ps, 1)
            pe.wait_ge(heads_ok, B + 1)

            pe.wait_ge(nan_cnt, 1)
            mm(bank[0][:, 0:B * GROUPS], ones[:, :], flag[0:KP, 0:B * GROUPS]).then_inc(nan_ps, 1)
            pe.wait_ge(nan_ok, 1)

            with pe.Fori(0, B // 2) as it:
                for p in range(2):
                    b = it * 2 + p
                    pe.wait_ge(att_ok, b + 1)
                    pe.wait_ge(y_ok, 2 * it + 1)
                    for k in range(DK):
                        last = turn(bank[4 * p][:, k * N:(k + 1) * N], att[p][0:N, k * 128:(k + 1) * 128], ident[0:N, 0:N])
                    last.then_inc(aT_ps, 1)
                for p in range(2):
                    b = it * 2 + p
                    pe.wait_ge(aT_ok, b + 1)
                    for k in range(DK):
                        last = mm(bank[4 * p + 1][0:N, 0:D], attT[p][:, k, :], xwo[:, k, :], start=(k == 0), stop=(k == DK - 1))
                    last.then_inc(wo_ps, 1)
                for p in range(2):
                    b = it * 2 + p
                    pe.wait_ge(xq_ok, b + 1)
                    for k in range(DK):
                        last = turn(bank[4 * p][:, k * N:(k + 1) * N], xq[p][0:N, k * 128:(k + 1) * 128], ident[0:N, 0:N])
                    last.then_inc(xqT_ps, 1)
                for p in range(2):
                    b = it * 2 + p
                    pe.wait_ge(xqT_ok, b + 1)
                    for w, (W, s) in enumerate(((wgT, gate_ps), (wuT, up_ps))):
                        for u in range(2):
                            for k in range(DK):
                                last = mm(bank[4 * p + 2 * w + u][0:N, 0:FF // 2], xqT[p][:, k, :], W[:, k, u * FF // 2:(u + 1) * FF // 2],
                                          start=(k == 0), stop=(k == DK - 1))
                        last.then_inc(s, 1)
                for p in range(2):
                    b = it * 2 + p
                    pe.wait_ge(hq_ok, b + 1)
                    for c, (o, m) in enumerate(FT):
                        last = turn(bank[4 * p + c // 4][0:m, (c % 4) * N:(c % 4 + 1) * N], hq[p][0:N, o:o + m], ident[0:N, 0:N])
                    last.then_inc(hqT_ps, 1)
                for p in range(2):
                    b = it * 2 + p
                    pe.wait_ge(hqT_ok, b + 1)
                    for c, (o, m) in enumerate(FT):
                        last = mm(bank[4 * p + 2][0:N, 0:D], hqT[p][0:m, c, :], wdT[0:m, c, :], start=(c == 0), stop=(c == len(FT) - 1))
                    last.then_inc(dn_ps, 1)

        @block.scalar
        def _(act):
            def copy(o, i):
                return nc.scalar.copy(o, i)

            n = 0
            for w, WT in enumerate((wgT, wuT)):
                for k in range(DK):
                    for jh in range(2):
                        act.wait_ge(w_turned, n + 1)
                        copy(WT[:, k, jh * 352:(jh + 1) * 352], bank[n % 8][:, 0:352]).then_inc(w_kept, 1)
                        n += 1
            for c, (o, m) in enumerate(FT):
                act.wait_ge(w_turned, n + 1)
                copy(wdT[0:m, c, :], bank[n % 8][0:m, 0:D]).then_inc(w_kept, 1)
                n += 1

            with act.Fori(0, B // 2) as it:
                for p in range(2):
                    b = it * 2 + p
                    act.wait_ge(xT_ps, b + 1)
                    copy(xsT[p][:], bank[4 * p][:, 0:DK * N].rearrange("p (k n) -> p k n", n=N)).then_inc(xT_ok, 1)
                for p in range(2):
                    b = it * 2 + p
                    act.wait_ge(v_ps, b + 1)
                    copy(vs[p][:], bank[4 * p + 2][0:N, 0:D]).then_inc(v_ok, 1)
                for p in range(2):
                    b = it * 2 + p
                    act.wait_ge(s_max, b + 1)
                    nc.scalar.activation(pr[p], sc[p], ACT.Exp, bias=row[p][:, 0:1], accum_out=row[p][:, 1:2]).then_inc(p_ok, 1)
                for p in range(2):
                    b = it * 2 + p
                    act.wait_ge(pT_ps, b + 1)
                    copy(prT[p], bank[4 * p][0:N, 0:N]).then_inc(pT_ok, 1)
                for p in range(2):
                    b = it * 2 + p
                    act.wait_ge(hT_ps, b + 1)
                    copy(xsT[p][:], bank[4 * p][:, 0:DK * N].rearrange("p (k n) -> p k n", n=N)).then_inc(hT_ok, 1)
                for p in range(2):
                    b = it * 2 + p
                    act.wait_ge(x1T_ps, b + 1)
                    copy(x1T[:, :, bass.ds(b * N, N)], bank[4 * p][:, 0:DK * N].rearrange("p (k n) -> p k n", n=N)).then_inc(x1T_ok, 1)

            act.wait_ge(cross_w, 16 * 9)
            act.wait_ge(scaled, 2)
            with act.Fori(0, B // 2) as it:
                for p in range(2):
                    b = it * 2 + p
                    act.wait_ge(cT_ps, b + 2)
                    for k in range(2):
                        last = nc.scalar.activation(cxT[p][:, k, :], bank[k][0:CK, 0:NK], ACT.Identity, accum_out=cxsum[p][:, k:k + 1])
                    last.then_inc(cT_ok, 1)
                    act.wait_ge(to_dram[p], 16 * it + 16)
                    for m in range(DK):
                        act.wait_ge(k_ps, DK * b + m + 1)
                        nc.scalar.activation(parts[p][:, 0, m, 0:NK], bank[m][:, 0:NK], ACT.Identity, bias=bkT[:, m:m + 1]).then_inc(k_hi, 1)
                    act.wait_ge(vx_ok, b + 1)
                    for m in range(DK):
                        nc.scalar.activation(parts[p][:, 0, m, NK:NK + N], bank[1][:, D + m * N:D + (m + 1) * N], ACT.Identity,
                                             bias=bqT[:, m:m + 1]).then_inc(q_hi, 1)
                    act.wait_ge(vm_ps, b + 1)
                    for m in range(DK):
                        last = nc.scalar.activation(vmeanT[:, m, bass.ds(b, 1)], bank[0][:, m:m + 1], ACT.Identity, bias=bvT[:, m:m + 1], scale=1.0 / NK)
                    last.then_inc(vm_ok, 1)
                for p in range(2):
                    b = it * 2 + p
                    act.wait_ge(neg_ok, b + 1)
                    nc.scalar.activation(floor[p][:], nmx[p][:, 0:H], ACT.Exp, bias=clampc[:, :]).then_inc(floor_ok, 1)
                    act.wait_ge(mT_ps, b + 1)
                    act.wait_ge(mrow_in[p], 16 * SHIFT * it + 16)
                    act.wait_ge(floor_out[p], 16 * it + 16)
                    copy(mrow[p][:], bank[7][0:3 * H, 0:N // 2].bitcast(BF16))
                    copy(floorT[p][:], bank[7][0:H, 256:256 + N]).then_inc(mT_ok, 1)
                for p in range(2):
                    b = it * 2 + p
                    for i in range(4):
                        act.wait_ge(prob_free, 4 * b + i + 1)
                        for c in range(KC):
                            g = i * KC + c
                            act.wait_ge(st_ps, b * GROUPS + g + 1)
                            nc.scalar.activation(prob[i][0:KP, c, :], bank[4 + g % 2][0:KP, 0:4 * N], ACT.Exp,
                                                 accum_out=wsum[:, bass.ds(b * GROUPS + g, 1)]).then_inc(exp_ok, 1)
                    act.wait_ge(prob_free, 4 * (b + 1) + 4)
                    act.wait_ge(o_ps, b - 1 + 2)
                    copy(oT[p][:], bank[6][:, 0:4 * N].rearrange("p (i n) -> p i n", n=N)).then_inc(oT_ok, 1)

            with act.Fori(0, B // 2) as it:
                for p in range(2):
                    b = it * 2 + p
                    act.wait_ge(heads_ok, B + 1)
                    act.wait_ge(nan_ok, 1)
                    act.wait_ge(aT_ps, 2 * it + 1)
                    copy(att[p][0:N], heads[:, b, :]).then_inc(att_ok, 1)
                for p in range(2):
                    b = it * 2 + p
                    act.wait_ge(aT_ps, b + 2)
                    copy(attT[p], bank[4 * p][:, 0:DK * N].rearrange("p (k n) -> p k n", n=N)).then_inc(aT_cp, 1)
                for p in range(2):
                    b = it * 2 + p
                    act.wait_ge(xqT_ps, b + 1)
                    copy(xqT[p], bank[4 * p][:, 0:DK * N].rearrange("p (k n) -> p k n", n=N)).then_inc(xqT_ok, 1)
                for p in range(2):
                    b = it * 2 + p
                    act.wait_ge(gate_ps, b + 1)
                    for u in range(2):
                        last = nc.scalar.activation(hat[p][0:N, u * FF // 2:(u + 1) * FF // 2], bank[4 * p + u][0:N, 0:FF // 2], ACT.Silu)
                    last.then_inc(silu_ok, 1)
                for p in range(2):
                    b = it * 2 + p
                    act.wait_ge(hqT_ps, b + 1)
                    copy(hqT[p][:, 0:4, :], bank[4 * p][:, 0:4 * N].rearrange("p (c n) -> p c n", n=N))
                    copy(hqT[p][:, 4, :], bank[4 * p + 1][:, 0:N])
                    copy(hqT[p][0:64, 5, :], bank[4 * p + 1][0:64, N:2 * N]).then_inc(hqT_ok, 1)

        @block.vector
        def _(dve):
            def quantise(steps, P, src, sc_, rs, t0, t1, dst):
                nb = src.free_size() // BLK
                blocks = lambda a: a.rearrange("p (b e) -> p b e", e=BLK)
                wide = lambda a: a.unsqueeze(2).broadcast_to([P, nb, BLK])
                v = nc.vector
                v.tensor_reduce(sc_, blocks(src), X, ALU.max, apply_absolute_value=True).then_inc(dve_step, 1)
                dve.wait_ge(dve_step, steps.next())
                v.tensor_scalar(sc_, sc_, 1.0 / 6.0, 1e-12, ALU.mult, ALU.max).then_inc(dve_step, 1)
                dve.wait_ge(dve_step, steps.next())
                v.reciprocal(rs, sc_).then_inc(dve_step, 1)
                dve.wait_ge(dve_step, steps.next())
                v.tensor_scalar(rs, rs, 1.0 - 2.0 ** -22, None, ALU.mult).then_inc(dve_step, 1)
                dve.wait_ge(dve_step, steps.next())
                v.tensor_scalar(t0.bitcast(U32), src.bitcast(U32), 0x7FFFFFFF, None, ALU.bitwise_and).then_inc(dve_step, 1)
                dve.wait_ge(dve_step, steps.next())
                v.tensor_tensor(blocks(t0), blocks(t0), wide(rs), ALU.mult).then_inc(dve_step, 1)
                dve.wait_ge(dve_step, steps.next())
                v.tensor_scalar(t1, t0, 1.0, HALF_UP, ALU.max, ALU.mult).then_inc(dve_step, 1)
                dve.wait_ge(dve_step, steps.next())
                v.tensor_tensor(t0, t0, t1, ALU.add).then_inc(dve_step, 1)
                dve.wait_ge(dve_step, steps.next())
                v.tensor_tensor(t0, t0, t1, ALU.subtract).then_inc(dve_step, 1)
                dve.wait_ge(dve_step, steps.next())
                v.tensor_tensor(blocks(t1), blocks(t0), wide(sc_), ALU.mult).then_inc(dve_step, 1)
                dve.wait_ge(dve_step, steps.next())
                return v.scalar_tensor_tensor(out=dst.bitcast(U32), in0=src.bitcast(U32), scalar=0x80000000, in1=t1.bitcast(U32),
                                              op0=ALU.bitwise_and, op1=ALU.bitwise_or)

            steps = Steps()
            dve.wait_ge(ffn_w, 48)
            for raw, P, L in ((raw_g, WP, WJ * D), (raw_u, WP, WJ * D), (raw_d, 128, 2 * FF)):
                flat = raw[0:P].rearrange("p j k -> p (j k)")
                s = scale[0][0:P, 0:L // BLK]
                r = scale[1][0:P, 0:L // BLK]
                quantise(steps, P, flat, s, r, tmp[0][0:P, 0:L], tmp[1][0:P, 0:L], flat).then_inc(w_quant, 1)
            dve.wait_ge(cross_w, 16 * 9)
            dve.wait_ge(consts, 1)
            nc.vector.tensor_scalar(xwq[:], xwq[:], HD ** -0.5, None, ALU.mult).then_inc(scaled, 1)
            nc.vector.tensor_scalar(bqT[:], bqT[:], HD ** -0.5, None, ALU.mult).then_inc(scaled, 1)
            dve.wait_ge(w_kept, 14)
            for p in range(2):
                last = nc.vector.memset(kst[p][ROWS:ROWS + SHIFT], 1.0)
            last.then_inc(w_kept, 1)

            def centre(steps, p, y, P):
                nc.vector.bn_stats(st6[p][0:P], y).then_inc(dve_step, 1)
                dve.wait_ge(dve_step, steps.next())
                dve.sem_inc(waits_met, 1)
                return nc.vector.bn_aggr(mv[p][0:P], st6[p][0:P])

            dve.wait_ge(self_w, 16 * 7)
            base = steps.n
            STEPS = 18
            with dve.Fori(0, B // 2) as it:
                steps = Steps(it * STEPS + base)
                for p in range(2):
                    b = it * 2 + p
                    dve.wait_ge(qk_ps, b + 1)
                    nc.vector.tensor_copy(qkT[p][:], bank[4 * p + 1][:, 0:4 * N].rearrange("p (k n) -> p k n", n=N)).then_inc(qk_ok, 1)
                for p in range(2):
                    b = it * 2 + p
                    dve.wait_ge(s_ps, b + 1)
                    nc.vector.scalar_tensor_tensor(out=sc[p], in0=bank[4 * p + 3][0:N, 0:N], scalar=D ** -0.5, in1=causal[:],
                                                           op0=ALU.mult, op1=ALU.add).then_inc(dve_step, 1)
                    dve.wait_ge(dve_step, steps.next())
                    nc.vector.tensor_reduce(row[p][:, 0:1], sc[p], X, ALU.max, negate=True).then_inc(s_max, 1)
                for p in range(2):
                    b = it * 2 + p
                    dve.wait_ge(p_ok, b + 1)
                    nc.vector.reciprocal(row[p][:, 2:3], row[p][:, 1:2]).then_inc(dve_step, 1)
                    dve.wait_ge(dve_step, steps.next())
                    dve.wait_ge(pv_ps, b + 1)
                    dve.wait_ge(v_ok, b + 1)
                    nc.vector.scalar_tensor_tensor(out=hs[p], in0=bank[4 * p + 1][0:N, 0:D], scalar=row[p][:, 2:3], in1=vs[p][:],
                                                           op0=ALU.mult, op1=ALU.add).then_inc(dve_step, 1)
                    dve.wait_ge(dve_step, steps.next())
                    centre(steps, p, hs[p], N).then_inc(var_ok, 1)
                for p in range(2):
                    b = it * 2 + p
                    dve.wait_ge(rstd_ok, 4 * it + p + 1)
                    nc.vector.tensor_scalar(hs[p], hs[p], mv[p][:, 0:1], rstd[p][:, 1:2], ALU.subtract, ALU.mult).then_inc(dve_step, 1)
                    dve.wait_ge(dve_step, steps.next())
                    nc.vector.tensor_tensor(hs[p], hs[p], gamma_b[:], ALU.mult).then_inc(dve_step, 1)
                    dve.wait_ge(dve_step, steps.next())
                    nc.vector.tensor_tensor(hs[p], hs[p], beta_b[:], ALU.add).then_inc(h_ok, 1)
                for p in range(2):
                    b = it * 2 + p
                    dve.wait_ge(fc_ps, b + 1)
                    nc.vector.tensor_tensor(x1s[p], bank[4 * p + 1][0:N, 0:D], xs[p][:], ALU.add).then_inc(dve_step, 1)
                    dve.wait_ge(dve_step, steps.next())
                    nc.vector.tensor_tensor(x1s[p], x1s[p], bfc_b[:], ALU.add).then_inc(dve_step, 1)
                    dve.wait_ge(dve_step, steps.next())
                    centre(steps, p, x1s[p], N).then_inc(var_ok, 1)
                for p in range(2):
                    b = it * 2 + p
                    dve.wait_ge(rstd_ok, 4 * it + 2 + p + 1)
                    nc.vector.tensor_scalar(x1[:, b, :], x1s[p], mv[p][:, 0:1], rstd[p][:, 1:2], ALU.subtract, ALU.mult)
                    nc.vector.tensor_scalar(x1s[p], x1s[p], mv[p][:, 0:1], rstd[p][:, 1:2], ALU.subtract, ALU.mult).then_inc(x1_ok, 1)
            assert steps.n == STEPS
            base += B // 2 * STEPS
            CS = 8
            with dve.Fori(0, B // 2) as it:
                steps = Steps(it * CS + base)
                for p in range(2):
                    b = it * 2 + p
                    dve.wait_ge(split_ok, 4 * 2 * it + 1)
                    for m in range(DK):
                        dve.wait_ge(k_hi, DK * b + m + 1)
                        nc.vector.scalar_tensor_tensor(out=rest[p][:, m, 0:NK], in0=bank[m][:, 0:NK], scalar=bkT[:, m:m + 1],
                                                       in1=parts[p][:, 0, m, 0:NK], op0=ALU.add, op1=ALU.subtract).then_inc(k_rest, 1)
                    dve.wait_ge(vq_ps, b + 1)
                    dve.wait_ge(prob_free, 8 * it + 4)
                    for c in range(KC):
                        last = nc.vector.tensor_tensor(vx[p][:, c, :, 0:HD], bank[c // 2][0:KP, (c % 2) * D:(c % 2 + 1) * D].rearrange("p (h d) -> p h d", d=HD),
                                                       bv_b[:].rearrange("p (h d) -> p h d", d=HD), ALU.add)
                    last.then_inc(vx_ok, 1)
                    for m in range(DK):
                        dve.wait_ge(q_hi, DK * b + m + 1)
                    for m in range(DK):
                        last = nc.vector.scalar_tensor_tensor(out=rest[p][:, m, NK:NK + N], in0=bank[1][:, D + m * N:D + (m + 1) * N], scalar=bqT[:, m:m + 1],
                                                              in1=parts[p][:, 0, m, NK:NK + N], op0=ALU.add, op1=ALU.subtract)
                    last.then_inc(q_rest, 1)
                for p in range(2):
                    b = it * 2 + p
                    for h in range(H):
                        dve.wait_ge(sx_ps, b * H + h + 1)
                        nc.vector.tensor_reduce(nmx[p][:, H + h:H + h + 1], bank[2 + h % 2][0:N, 0:NK], X, ALU.max, negate=True).then_inc(sx_max, 1)
                    dve.wait_ge(sx_max, (b + 1) * H + 2)
                    nc.vector.tensor_scalar(nmx[p][:, 0:H], nmx[p][:, H:2 * H], CLAMP, -CLAMP, ALU.min, ALU.max).then_inc(neg_ok, 1)
                    dve.wait_ge(neg_ok, b + 1)
                    nc.vector.tensor_copy(mparts[p][:, 0, :], nmx[p][:, 0:H]).then_inc(dve_step, 1)
                    dve.wait_ge(dve_step, steps.next())
                    nc.vector.tensor_tensor(nmx[p][:, H:2 * H], nmx[p][:, 0:H], mparts[p][:, 0, :], ALU.subtract).then_inc(dve_step, 1)
                    dve.wait_ge(dve_step, steps.next())
                    nc.vector.tensor_copy(mparts[p][:, 1, :], nmx[p][:, H:2 * H]).then_inc(dve_step, 1)
                    dve.wait_ge(dve_step, steps.next())
                    nc.vector.tensor_tensor(mparts[p][:, 2, :], nmx[p][:, H:2 * H], mparts[p][:, 1, :], ALU.subtract).then_inc(mparts_ok, 1)
                for p in range(2):
                    b = it * 2 + p
                    dve.wait_ge(floor_in[p], 16 * (it + 1))
                    for i in range(4):
                        dve.wait_ge(exp_ok, b * GROUPS + KC * (i + 1) + 2)
                        fl = floor_b[:, 4 * i * N:4 * (i + 1) * N].unsqueeze(1).broadcast_to([KP, KC, 4 * N])
                        nc.vector.scalar_tensor_tensor(out=prob[i][0:KP], in0=prob[i][0:KP], scalar=1.0, in1=fl, op0=ALU.min, op1=ALU.max).then_inc(clip_ok, 1)
                    dve.wait_ge(o_ps, b + 2)
                    o4 = bank[7][0:N, :].rearrange("q (h e) -> q h e", e=32)
                    nc.vector.reciprocal(rden[p][:], o4[:, :, HD]).then_inc(dve_step, 1)
                    dve.wait_ge(dve_step, steps.next())
                    nc.vector.tensor_tensor(heads[:, b, :].rearrange("q (h d) -> q h d", d=HD), o4[:, :, 0:HD],
                                            rden[p][:].unsqueeze(2).broadcast_to([N, H, HD]), ALU.mult).then_inc(heads_ok, 1)
            assert steps.n == CS
            base += B // 2 * CS
            steps = Steps(base)
            dve.wait_ge(exp_ok, B * GROUPS + 2)
            nc.vector.tensor_tensor(flag[0:KP, 0:B * GROUPS], wsum[:, :], wsum[:, :], ALU.not_equal).then_inc(nan_cnt, 1)
            dve.wait_ge(nan_ps, 1)
            nc.vector.tensor_reduce(flag[:, B * GROUPS:B * GROUPS + 1], bank[0][:, 0:B * GROUPS], X, ALU.max).then_inc(dve_step, 1)
            dve.wait_ge(dve_step, steps.next())
            nc.vector.tensor_scalar(nanmask[:, :], flag[:, B * GROUPS:B * GROUPS + 1], 0.0, None, ALU.is_gt).then_inc(nan_ok, 1)
            dve.wait_ge(nan_ok, 1)
            base += steps.n
            FS = 58
            with dve.Fori(0, B // 2) as it:
                steps = Steps(it * FS + base)
                for p in range(2):
                    b = it * 2 + p
                    dve.wait_ge(aT_cp, b + 1)
                    nc.vector.tensor_copy(vmean[p][:, :, :], vmeanT[:, :, bass.ds(b, 1)]).then_inc(dve_step, 1)
                    dve.wait_ge(dve_step, steps.next())
                    dve.sem_inc(waits_met, 1)
                    for k in range(DK):
                        last = nc.vector.copy_predicated(attT[p][:, k, :], nanmask[:, 0:1].broadcast_to([128, N]),
                                                         vmean[p][:, k, :].broadcast_to([128, N]))
                    last.then_inc(aT_ok, 1)
                for p in range(2):
                    b = it * 2 + p
                    dve.wait_ge(wo_ps, b + 1)
                    nc.vector.tensor_tensor(x2[p][0:N], bank[4 * p + 1][0:N, 0:D], bo_b[:], ALU.add).then_inc(dve_step, 1)
                    dve.wait_ge(dve_step, steps.next())
                    nc.vector.tensor_tensor(x2[p][0:N], x2[p][0:N], x1[:, b, :], ALU.add).then_inc(dve_step, 1)
                    dve.wait_ge(dve_step, steps.next())
                    centre(steps, p, x2[p][0:N], N).then_inc(varf, 1)
                for p in range(2):
                    b = it * 2 + p
                    dve.wait_ge(rstdf, 4 * it + p + 1)
                    nc.vector.tensor_scalar(x2[p][0:N], x2[p][0:N], mv[p][:, 0:1], rstd[p][:, 1:2], ALU.subtract, ALU.mult).then_inc(dve_step, 1)
                    dve.wait_ge(dve_step, steps.next())
                    nb = D // BLK
                    quantise(steps, N, x2[p][0:N], scale[p][0:N, 0:nb], scale[p][0:N, 128:128 + nb], ft[p][0][0:N, 0:D], ft[p][1][0:N, 0:D],
                             xq[p][0:N]).then_inc(xq_ok, 1)
                for p in range(2):
                    b = it * 2 + p
                    dve.wait_ge(silu_ok, b + 1)
                    dve.wait_ge(up_ps, b + 1)
                    for u in range(2):
                        half = hat[p][0:N, u * FF // 2:(u + 1) * FF // 2]
                        nc.vector.tensor_tensor(half, half, bank[4 * p + 2 + u][0:N, 0:FF // 2], ALU.mult).then_inc(dve_step, 1)
                        dve.wait_ge(dve_step, steps.next())
                    nb = FF // BLK
                    quantise(steps, N, hat[p][0:N], scale[p][0:N, 0:nb], scale[p][0:N, 128:128 + nb], ft[p][0][0:N], ft[p][1][0:N],
                             hq[p][0:N]).then_inc(hq_ok, 1)
                for p in range(2):
                    b = it * 2 + p
                    dve.wait_ge(dn_ps, b + 1)
                    dve.wait_ge(y_out[p], 16 * it + 16)
                    nc.vector.tensor_tensor(yo[p][0:N], bank[4 * p + 2][0:N, 0:D], x2[p][0:N], ALU.add).then_inc(dve_step, 1)
                    dve.wait_ge(dve_step, steps.next())
                    centre(steps, p, yo[p][0:N], N).then_inc(varf, 1)
                for p in range(2):
                    b = it * 2 + p
                    dve.wait_ge(rstdf, 4 * it + 2 + p + 1)
                    nc.vector.tensor_scalar(yo[p][0:N], yo[p][0:N], mv[p][:, 0:1], rstd[p][:, 1:2], ALU.subtract, ALU.mult).then_inc(y_ok, 1)
            assert steps.n == FS

        @block.gpsimd
        def _(pool):
            for free, credit in credited:
                pool.sem_inc(free, credit)
            steps = Steps()
            for t in (ident, identb, causal):
                nc.gpsimd.memset(t[:], 0.0).then_inc(pool_step, 1)
                pool.wait_ge(pool_step, steps.next())
            for t in (ident, identb):
                nc.gpsimd.affine_select(out=t[:], in_=t[:], compare_op=ALU.not_equal, fill=1.0, base=0, pattern=[[-1, 128]], channel_multiplier=1).then_inc(pool_step, 1)
                pool.wait_ge(pool_step, steps.next())
            nc.gpsimd.affine_select(out=causal[:], in_=causal[:], compare_op=ALU.is_ge, fill=-3e38, base=0, pattern=[[-1, N]], channel_multiplier=1).then_inc(pool_step, 1)
            pool.wait_ge(pool_step, steps.next())
            nc.gpsimd.memset(mhalf[:], -0.5).then_inc(pool_step, 1)
            pool.wait_ge(pool_step, steps.next())
            nc.gpsimd.memset(clampc[:], -CLAMP).then_inc(pool_step, 1)
            pool.wait_ge(pool_step, steps.next())
            nc.gpsimd.memset(ones[:], 1.0).then_inc(pool_step, 1)
            pool.wait_ge(pool_step, steps.next())
            for p in range(2):
                nc.gpsimd.memset(vx[p][:], 0.0).then_inc(pool_step, 1)
                pool.wait_ge(pool_step, steps.next())
                nc.gpsimd.memset(vx[p][:, :, :, HD:HD + 1], 1.0).then_inc(pool_step, 1)
                pool.wait_ge(pool_step, steps.next())
            nc.gpsimd.memset(flag[:, B * GROUPS:], 0.0).then_inc(consts, 1)
            base = steps.n

            def root(steps, p):
                pool.sem_inc(waits_met, 1)
                nc.gpsimd.tensor_scalar(rstd[p][:, 0:1], mv[p][:, 1:2], EPS, None, ALU.add).then_inc(pool_step, 1)
                pool.wait_ge(pool_step, steps.next())
                return nc.gpsimd.tensor_tensor(rstd[p][:, 1:2], rstd[p][:, 0:1], mhalf[0:N, :], ALU.pow)

            with pool.Fori(0, B // 2) as it:
                steps = Steps(it * 4 + base)
                for r in range(2):
                    for p in range(2):
                        pool.wait_ge(var_ok, 4 * it + 2 * r + p + 1)
                        root(steps, p).then_inc(rstd_ok, 1)
            base += B // 2 * 4
            with pool.Fori(0, B // 2) as it:
                steps = Steps(it * 8 + base)
                for p in range(2):
                    b = it * 2 + p
                    pool.wait_ge(to_dram[p], 16 * it + 16)
                    for m in range(DK):
                        pool.wait_ge(k_rest, DK * b + m + 1)
                        pool.sem_inc(waits_met, 1)
                        nc.gpsimd.tensor_copy(parts[p][:, 1, m, 0:NK], rest[p][:, m, 0:NK]).then_inc(pool_step, 1)
                        pool.wait_ge(pool_step, steps.next())
                        nc.gpsimd.tensor_tensor(parts[p][:, 2, m, 0:NK], rest[p][:, m, 0:NK], parts[p][:, 1, m, 0:NK], ALU.subtract).then_inc(split_ok, 1)
                    pool.wait_ge(q_rest, b + 2)
                    for m in range(DK):
                        pool.sem_inc(waits_met, 1)
                        nc.gpsimd.tensor_copy(parts[p][:, 1, m, NK:NK + N], rest[p][:, m, NK:NK + N]).then_inc(pool_step, 1)
                        pool.wait_ge(pool_step, steps.next())
                        nc.gpsimd.tensor_tensor(parts[p][:, 2, m, NK:NK + N], rest[p][:, m, NK:NK + N], parts[p][:, 1, m, NK:NK + N],
                                                ALU.subtract).then_inc(split_ok, 1)
            base += B // 2 * 8
            with pool.Fori(0, B // 2) as it:
                steps = Steps(it * 4 + base)
                for r in range(2):
                    for p in range(2):
                        pool.wait_ge(varf, 4 * it + 2 * r + p + 1)
                        root(steps, p).then_inc(rstdf, 1)


_INS = ['x', 'ctx_768', 'L0_attn_Wq', 'L0_attn_Wk', 'L0_attn_Wv', 'L0_attn_Wfc', 'L0_attn_bfc', 'L0_attn_gamma', 'L0_attn_beta',
        'L0_xattn_Wq', 'L0_xattn_bq', 'L0_xattn_Wk', 'L0_xattn_bk', 'L0_xattn_Wv', 'L0_xattn_bv', 'L0_xattn_Wo', 'L0_xattn_bo',
        'L0_ffn_w_gate', 'L0_ffn_w_up', 'L0_ffn_w_down']
_OUTS = [((16, 112, 256), 'float32')]


def kernel(**inputs):
    import numpy as _np
    import concourse.bacc as _bacc
    from concourse import mybir as _mybir
    from concourse.bass_utils import run_bass_kernel_spmd as _run

    nc = _bacc.Bacc("TRN2", target_bir_lowering=False, num_devices=1)
    arrays, args = {}, []
    for name in _INS:
        a = _np.ascontiguousarray(inputs[name])
        arrays[f"in_{name}_dram"] = a
        args.append(nc.dram_tensor(f"in_{name}_dram", a.shape, _mybir.dt.from_np(a.dtype), kind="ExternalInput").ap())
    for i, (shape, dtype) in enumerate(_OUTS):
        dt = _mybir.dt.from_np(_np.dtype(dtype))
        args.append(nc.dram_tensor(f"out_{i}_dram", shape, dt, kind="ExternalOutput").ap())
    decoder_layer(nc, *args)
    r = _run(nc, [arrays], core_ids=[0])
    got = tuple(r.results[0][f"out_{i}_dram"] for i in range(len(_OUTS)))
    return got[0]
```

```python
from contextlib import ExitStack

import concourse.bass as bass
from concourse import mybir

F32 = mybir.dt.float32
BF16 = mybir.dt.bfloat16
U32 = mybir.dt.uint32
I32 = mybir.dt.int32
ALU = mybir.AluOpType
ACT = mybir.ActivationFunctionType
X = mybir.AxisListType.X

B, N, D = 16, 112, 256
NK, DC = 375, 192
H, HD = 16, 16
FF, BLK = 704, 16
KC, KP = 3, 125
DK = D // 128
CK = DC // 2
WP, WJ = 88, 8
FT = [(c * 128, min(128, FF - c * 128)) for c in range((FF + 127) // 128)]
TERMS = [(0, 3), (1, 2), (2, 1)]
ROWS = 16 * sum(n for _, n in TERMS)
SHIFT = 3
CLAMP = 10000.0
EPS = 1e-5
GROUPS = 4 * KC
HALF_UP = 4194304.0
LOOPED = B - 6


def seq(it, s):
    return it * 2 + s, it + s // 2, s % 2


class Steps:

    def __init__(self, base=0):
        self.base, self.n = base, 0

    def next(self):
        self.n += 1
        return self.base + self.n


def decoder_layer(nc, x, ctx_in, Wq, Wk, Wv, Wfc, bfc, gamma, beta, xWq, xbq, xWk, xbk, xWv, xbv, xWo, xbo,
                  w_gate, w_up, w_down, out):
    ctx = ExitStack()
    with ctx:
        def sb(name, shape, dt=F32):
            return ctx.enter_context(nc.sbuf_tensor(name, shape, dt))

        credited = []

        def sem(name, credit=0):
            made = ctx.enter_context(nc.semaphore(name))
            if credit:
                credited.append((made, credit))
            return made

        def two(name, credit=0):
            return [sem(f"{name}{p}", credit) for p in range(2)]

        ident = sb("ident", [128, 128])
        identb = sb("identb", [128, 128], BF16)
        x1 = sb("x1", [N, B, D])
        x1T = sb("x1T", [128, DK, B * N])
        heads = sb("heads", [N, B, D])
        vmeanT = sb("vmeanT", [128, DK, B])
        wsum = sb("wsum", [KP, B * GROUPS])
        wq, wk, wv, wfc = (sb(n, [128, DK, D]) for n in ("wq", "wk", "wv", "wfc"))
        xwq, xwo = (sb(n, [128, DK, D]) for n in ("xwq", "xwo"))
        xwk, xwv = (sb(n, [CK, 2, D]) for n in ("xwk", "xwv"))
        bfc_b, gamma_b, beta_b, bo_b = (sb(n, [N, D]) for n in ("bfc_b", "gamma_b", "beta_b", "bo_b"))
        bv_b = sb("bv_b", [KP, D])
        bqT, bkT, bvT = (sb(n, [128, DK]) for n in ("bqT", "bkT", "bvT"))
        wgT, wuT = sb("wgT", [128, DK, FF]), sb("wuT", [128, DK, FF])
        wdT = sb("wdT", [128, len(FT), D])
        causal = sb("causal", [N, N])
        mhalf = sb("mhalf", [128, 1])
        clampc = sb("clampc", [N, 1])

        arena = sb("arena", [128, 12288])
        place = [0]

        def carve(words):
            place[0] += words
            assert place[0] <= 12288
            return arena[:, place[0] - words:place[0]]

        raw_g = carve(WJ * D).rearrange("p (j k) -> p j k", k=D)
        raw_u = carve(WJ * D).rearrange("p (j k) -> p j k", k=D)
        raw_d = carve(2 * FF).rearrange("p (j k) -> p j k", k=FF)
        tmp = [carve(WJ * D) for _ in range(3)]
        place[0] = 0
        kst = [carve(H * NK // 2).bitcast(BF16).rearrange("p (h k) -> p h k", k=NK) for _ in range(2)]
        prob = [carve(KC * 4 * N).rearrange("p (c n) -> p c n", c=KC) for _ in range(4)]
        place[0] = 0
        hat = [carve(FF) for _ in range(2)]
        hq = [carve(FF) for _ in range(2)]
        ft = [[carve(FF) for _ in range(2)] for _ in range(2)]
        hqT = [carve(len(FT) * N).rearrange("p (c n) -> p c n", n=N) for _ in range(2)]
        att = [carve(D) for _ in range(2)]
        attT = [carve(DK * N).rearrange("p (k n) -> p k n", n=N) for _ in range(2)]
        x2 = [carve(D) for _ in range(2)]
        xq = [carve(D) for _ in range(2)]
        xqT = [carve(DK * N).rearrange("p (k n) -> p k n", n=N) for _ in range(2)]
        yo = [carve(D) for _ in range(2)]

        xs = [sb(f"xs{p}", [N, D]) for p in range(2)]
        xsT = [sb(f"xsT{p}", [128, DK, N]) for p in range(2)]
        qkT = [sb(f"qkT{p}", [128, 2 * DK, N]) for p in range(2)]
        vs = [sb(f"vs{p}", [N, D]) for p in range(2)]
        rest = [sb(f"rest{p}", [128, DK, NK + N]) for p in range(2)]
        lend = [r[0:N].rearrange("p k n -> p (k n)") for r in rest]
        sc, pr, prT = ([r[:, i * N:(i + 1) * N] for r in lend] for i in range(3))
        hs, x1s = ([r[:, 3 * N + i * D:3 * N + (i + 1) * D] for r in lend] for i in range(2))
        row = [sb(f"row{p}", [N, 4]) for p in range(2)]
        st6 = [sb(f"st6{p}", [N, 6]) for p in range(2)]
        mv = [sb(f"mv{p}", [N, 2]) for p in range(2)]
        rstd = [sb(f"rstd{p}", [N, 2]) for p in range(2)]

        cx = [sb(f"cx{p}", [KP, KC, DC]) for p in range(2)]
        cxsum = [sb(f"cxsum{p}", [CK, 2]) for p in range(2)]
        cxT = [sb(f"cxT{p}", [CK, 2, NK]) for p in range(2)]
        parts_flat = [sb(f"parts{p}", [128, 3 * DK * (NK + N)], BF16) for p in range(2)]
        parts = [t[:].rearrange("p (t m k) -> p t m k", t=3, m=DK) for t in parts_flat]
        by_head = [t[:, 0:2 * DK * D].bitcast(F32) for t in parts_flat]
        qst = [sb(f"qst{p}", [ROWS + SHIFT, H, N], BF16) for p in range(2)]
        vx = [sb(f"vx{p}", [KP, KC, H, 32]) for p in range(2)]
        nmx = [sb(f"nmx{p}", [N, 3 * H]) for p in range(2)]
        mparts = [sb(f"mparts{p}", [N, 3, H], BF16) for p in range(2)]
        floor = [sb(f"floor{p}", [N, H]) for p in range(2)]
        mrow = [sb(f"mrow{p}", [3 * H, N], BF16) for p in range(2)]
        floorT = [sb(f"floorT{p}", [H, N]) for p in range(2)]
        floor_b = sb("floor_b", [KP, H * N])
        oT = qkT
        rden = [sb(f"rden{p}", [N, H]) for p in range(2)]
        scale = [sb(f"scale{p}", [128, 2 * 128]) for p in range(2)]
        flag = sb("flag", [128, B * GROUPS + 4])
        vmean = [sb(f"vmean{p}", [128, DK, 1]) for p in range(2)]
        nanmask = sb("nanmask", [128, 1], I32)
        ones = sb("ones", [KP, 128])

        k_dram = nc.dram_tensor("k_parts", [2, 3, 2, HD, H // 2, NK], BF16).ap()
        q_dram = nc.dram_tensor("q_parts", [2, 3, 2, HD, H // 2, N], BF16).ap()
        floor_dram = nc.dram_tensor("floor_rows", [2, H * N], F32).ap()

        ps = ctx.enter_context(nc.psum_tensor("ps", [128, 8 * 512], F32))
        bank = [ps[:, i * 512:(i + 1) * 512] for i in range(8)]

        self_w, cross_w, ffn_w = sem("self_w"), sem("cross_w"), sem("ffn_w")
        consts = sem("consts")
        waits_met = sem("waits_met")
        dve_step = sem("dve_step")
        pool_step = sem("pool_step")
        w_quant, w_turned, w_kept = sem("w_quant"), sem("w_turned"), sem("w_kept")
        scaled = sem("scaled")
        stacks_one = sem("stacks_one")
        x_in, xT_ps, xT_ok = two("x_in"), sem("xT_ps"), sem("xT_ok")
        qk_ps, qk_ok, v_ps, v_ok = sem("qk_ps"), sem("qk_ok"), sem("v_ps"), sem("v_ok")
        s_ps, s_max, p_ok, pT_ps, pT_ok = sem("s_ps"), sem("s_max"), sem("p_ok"), sem("pT_ps"), sem("pT_ok")
        pv_ps, var_ok, rstd_ok = sem("pv_ps"), sem("var_ok"), sem("rstd_ok")
        h_ok, hT_ps, hT_ok, fc_ps = sem("h_ok"), sem("hT_ps"), sem("hT_ok"), sem("fc_ps")
        x1_ok, x1T_ps, x1T_ok = sem("x1_ok", 1), sem("x1T_ps"), sem("x1T_ok", 1)

        c_in, cT_ps, cT_ok = two("c_in"), sem("cT_ps"), sem("cT_ok")
        k_ps, k_hi, k_rest = sem("k_ps"), sem("k_hi"), sem("k_rest")
        vx_ps, vx_ok, q_ps, q_hi, q_rest = sem("vx_ps"), sem("vx_ok"), sem("q_ps"), sem("q_hi"), sem("q_rest")
        vm_ps, vm_ok = sem("vm_ps"), sem("vm_ok")
        split_ok = sem("split_ok")
        to_dram = [two("to_dram_low"), two("to_dram_high")]
        stacked = [two("stacked_low"), two("stacked_high")]
        sx_ps, sx_max = sem("sx_ps"), sem("sx_max", 3)
        neg_ok, mparts_ok, floor_ok = sem("neg_ok"), sem("mparts_ok"), sem("floor_ok")
        mT_ps, mT_ok = sem("mT_ps"), sem("mT_ok")
        mrow_in, floor_out, floor_in = two("mrow_in", 16), two("floor_out", 16), two("floor_in")
        st_ps, exp_ok, clip_ok = sem("st_ps"), sem("exp_ok", 2), sem("clip_ok")
        prob_free = sem("prob_free", 4)
        oT_ok, o_ps, heads_ok = sem("oT_ok", 1), sem("o_ps"), sem("heads_ok")

        nan_cnt, nan_ps, nan_ok = sem("nan_cnt"), sem("nan_ps"), sem("nan_ok")
        att_ok, aT_ps, aT_cp, aT_ok = sem("att_ok"), sem("aT_ps", 1), sem("aT_cp"), sem("aT_ok")
        wo_ps, xq_ok, xqT_ps, xqT_ok = sem("wo_ps"), sem("xq_ok"), sem("xqT_ps"), sem("xqT_ok")
        gate_ps, up_ps, silu_ok, hq_ok = sem("gate_ps"), sem("up_ps"), sem("silu_ok"), sem("hq_ok")
        hqT_ps, hqT_ok, dn_ps, y_ok = sem("hqT_ps"), sem("hqT_ok"), sem("dn_ps"), sem("y_ok", 1)
        y_out = two("y_out", 16)
        varf, rstdf = sem("varf"), sem("rstdf")

        block = ctx.enter_context(nc.Block())

        @block.sync
        def _(sp):
            def rows_of(w):
                return w.rearrange("(k p) n -> p k n", p=128)

            sp.dma_start(wq[:], rows_of(Wq)).then_inc(self_w, 16)
            sp.dma_start(wk[:], rows_of(Wk)).then_inc(self_w, 16)
            sp.dma_start(wv[:], rows_of(Wv)).then_inc(self_w, 16)
            sp.dma_start(wfc[:], rows_of(Wfc)).then_inc(self_w, 16)
            sp.dma_start(bfc_b[:], bfc.partition_broadcast(N)).then_inc(self_w, 16)
            sp.dma_start(gamma_b[:], gamma.partition_broadcast(N)).then_inc(self_w, 16)
            sp.dma_start(beta_b[:], beta.partition_broadcast(N)).then_inc(self_w, 16)
            sp.dma_start(raw_g[0:WP], w_gate.rearrange("(j p) k -> p j k", p=WP)).then_inc(ffn_w, 16)
            sp.dma_start(raw_u[0:WP], w_up.rearrange("(j p) k -> p j k", p=WP)).then_inc(ffn_w, 16)
            sp.dma_start(raw_d, w_down.rearrange("(j p) k -> p j k", p=128)).then_inc(ffn_w, 16)
            sp.dma_start(by_head[0].rearrange("p (k n) -> p k n", k=DK), rows_of(xWq)).then_inc(cross_w, 16)
            sp.dma_start(xwo[:], rows_of(xWo)).then_inc(cross_w, 16)
            sp.dma_start(by_head[1][0:CK].rearrange("p (k n) -> p k n", k=2), xWk.rearrange("(k p) n -> p k n", p=CK)).then_inc(cross_w, 16)
            sp.dma_start(xwv[:], xWv.rearrange("(k p) n -> p k n", p=CK)).then_inc(cross_w, 16)
            sp.dma_start(bo_b[:], xbo.partition_broadcast(N)).then_inc(cross_w, 16)
            sp.dma_start(bv_b[:], xbv.partition_broadcast(KP)).then_inc(cross_w, 16)
            for k in range(DK):
                sp.dma_start(bqT[:, k:k + 1], xbq[k * 128:(k + 1) * 128].rearrange("(h d) -> d h", d=HD), allow_slow_non_contiguous=True).then_inc(cross_w, 16)
            sp.dma_start(bvT[:], xbv.rearrange("(k p) -> p k", p=128), allow_slow_non_contiguous=True).then_inc(cross_w, 16)
            for k in range(DK):
                sp.dma_start(bkT[:, k:k + 1], xbk[k * 128:(k + 1) * 128].rearrange("(h d) -> d h", d=HD), allow_slow_non_contiguous=True).then_inc(cross_w, 16)
            with sp.Fori(0, B // 2) as it:
                for p in range(2):
                    sp.wait_ge(x1_ok, 2 * it + 1)
                    sp.sem_inc(waits_met, 1)
                    sp.dma_start(xs[p][:], x[it * 2 + p]).then_inc(x_in[p], 16)
            def context(b, u, p):
                sp.dma_start(cx[p][:], ctx_in[b].rearrange("(p c) d -> p c d", c=KC)).then_inc(c_in[p], 16)

            def parts_out(b, u, p, half, first=False):
                sp.wait_ge(split_ok, 4 * b + 3 + half)
                sp.sem_inc(waits_met, 1)
                if not first:
                    sp.wait_ge(stacked[half][p], 16 * 6 * u)
                    sp.sem_inc(waits_met, 1)
                for to, of in ((k_dram, parts[p][:, :, half, 0:NK]), (q_dram, parts[p][:, :, half, NK:NK + N])):
                    sp.dma_start(to[p, :, half].rearrange("t d h k -> (d h) t k"), of).then_inc(to_dram[half][p], 16)

            def stacks_in(b, u, p, half, first=False):
                sp.wait_ge(to_dram[half][p], 32 * (u + 1))
                sp.sem_inc(waits_met, 1)
                if not first:
                    sp.wait_ge(exp_ok, GROUPS * (b - 2) + GROUPS // 2 * (half + 1) + 2)
                    sp.sem_inc(waits_met, 1)
                lo, hi, row = half * H // 2, (half + 1) * H // 2, 0
                for part, times in TERMS:
                    keys_of = k_dram[p, part, half].rearrange("d h k -> d (h k)").unsqueeze(0).broadcast_to([times, HD, H // 2 * NK])
                    queries_of = q_dram[p, 0:times, half].rearrange("t d h k -> t d (h k)")
                    sp.dma_start(kst[p][row:row + 16 * times, lo:hi, :], keys_of).then_inc(stacked[half][p], 16)
                    sp.dma_start(qst[p][row:row + 16 * times, lo:hi, :], queries_of).then_inc(stacked[half][p], 16)
                    row += 16 * times

            def rows_in(b, u, p):
                sp.wait_ge(mT_ok, b + 1)
                sp.sem_inc(waits_met, 1)
                sp.dma_start(qst[p][ROWS:ROWS + SHIFT], mrow[p][:]).then_inc(mrow_in[p], 16)

            def floor_rows_out(b, u, p):
                sp.dma_start(floor_dram[p].rearrange("(h q) -> h q", h=H), floorT[p][:]).then_inc(floor_out[p], 16)

            def floor_rows(b, u, p, first=False):
                sp.wait_ge(floor_out[p], 16 * (u + 1) + 16)
                sp.sem_inc(waits_met, 1)
                if not first:
                    sp.wait_ge(clip_ok, 4 * b)
                    sp.sem_inc(waits_met, 1)
                sp.dma_start(floor_b[:], floor_dram[p].partition_broadcast(KP)).then_inc(floor_in[p], 16)

            def cross_step(it, s):
                static = isinstance(it, int)
                if not static or s > 0:
                    floor_rows(*seq(it, s))
                    if not static or s + 1 < B:
                        stacks_in(*seq(it, s + 1), 1, first=static and s == 0)
                if not static or s + 4 < B:
                    sp.wait_ge(cT_ps, 2 * (it * 2 + s + 3))
                    sp.sem_inc(waits_met, 1)
                    context(*seq(it, s + 4))
                if not static or s + 2 < B:
                    parts_out(*seq(it, s + 2), 0)
                    stacks_in(*seq(it, s + 2), 0)
                    parts_out(*seq(it, s + 2), 1)
                if not static or s + 1 < B:
                    rows_in(*seq(it, s + 1))
                    floor_rows_out(*seq(it, s + 1))

            context(*seq(0, 0))
            context(*seq(0, 1))
            sp.wait_ge(cT_ps, 2)
            context(*seq(0, 2))
            sp.wait_ge(w_kept, 15)
            for s in range(2):
                for half in range(2):
                    parts_out(*seq(0, s), half, first=True)
                for half in range(2):
                    stacks_in(*seq(0, s), half, first=True)
            sp.wait_ge(cT_ps, 4)
            context(*seq(0, 3))
            rows_in(*seq(0, 0))
            floor_rows_out(*seq(0, 0))
            floor_rows(*seq(0, 0), first=True)
            cross_step(0, 0)
            with sp.Fori(0, LOOPED // 2) as it:
                for s in range(1, 3):
                    cross_step(it, s)
            for s in range(LOOPED + 1, B):
                cross_step(0, s)
            with sp.Fori(0, B // 2) as it:
                for p in range(2):
                    b = it * 2 + p
                    sp.wait_ge(y_ok, b + 2)
                    sp.sem_inc(waits_met, 1)
                    sp.dma_start(out[b], yo[p][0:N]).then_inc(y_out[p], 16)
            for p in range(2):
                sp.wait_ge(y_out[p], 16 * B // 2 + 16)
            sp.sem_inc(waits_met, 1)

        @block.tensor
        def _(pe):
            def mm(o, l, r, start=True, stop=True):
                return nc.tensor.matmul(o, l, r, start=start, stop=stop)

            def turn(o, i, idt):
                return nc.tensor.transpose(o, i, idt)

            pe.wait_ge(consts, 1)
            n = 0
            for w, raw in enumerate((raw_g, raw_u)):
                pe.wait_ge(w_quant, w + 1)
                for k in range(DK):
                    for jh in range(2):
                        if n >= 8:
                            pe.wait_ge(w_kept, n - 7)
                        for j in range(4):
                            last = turn(bank[n % 8][:, j * WP:(j + 1) * WP], raw[0:WP, jh * 4 + j, k * 128:(k + 1) * 128], ident[0:WP, 0:WP])
                        last.then_inc(w_turned, 1)
                        n += 1
            pe.wait_ge(w_quant, 3)
            for c, (o, m) in enumerate(FT):
                if n >= 8:
                    pe.wait_ge(w_kept, n - 7)
                for j in range(2):
                    last = turn(bank[n % 8][0:m, j * 128:(j + 1) * 128], raw_d[:, j, o:o + m], ident[:, :])
                last.then_inc(w_turned, 1)
                n += 1
            pe.wait_ge(w_kept, 14)

            pe.wait_ge(self_w, 16 * 7)
            with pe.Fori(0, B // 2) as it:
                for p in range(2):
                    b = it * 2 + p
                    pe.wait_ge(x_in[p], 16 * (it + 1))
                    pe.wait_ge(x1T_ok, 2 * it + 1)
                    for k in range(DK):
                        last = turn(bank[4 * p][:, k * N:(k + 1) * N], xs[p][:, k * 128:(k + 1) * 128], ident[0:N, 0:N])
                    last.then_inc(xT_ps, 1)
                for p in range(2):
                    b = it * 2 + p
                    pe.wait_ge(xT_ok, b + 1)
                    for w, W in enumerate((wq, wk)):
                        for m in range(DK):
                            for k in range(DK):
                                last = mm(bank[4 * p + 1][:, (w * DK + m) * N:(w * DK + m + 1) * N], W[:, k, m * 128:(m + 1) * 128],
                                          xsT[p][:, k, :], start=(k == 0), stop=(k == DK - 1))
                    last.then_inc(qk_ps, 1)
                    for k in range(DK):
                        last = mm(bank[4 * p + 2][0:N, 0:D], xsT[p][:, k, :], wv[:, k, :], start=(k == 0), stop=(k == DK - 1))
                    last.then_inc(v_ps, 1)
                for p in range(2):
                    b = it * 2 + p
                    pe.wait_ge(qk_ok, b + 1)
                    for k in range(DK):
                        last = mm(bank[4 * p + 3][0:N, 0:N], qkT[p][:, k, :], qkT[p][:, DK + k, :], start=(k == 0), stop=(k == DK - 1))
                    last.then_inc(s_ps, 1)
                for p in range(2):
                    b = it * 2 + p
                    pe.wait_ge(p_ok, b + 1)
                    turn(bank[4 * p][0:N, 0:N], pr[p], ident[0:N, 0:N]).then_inc(pT_ps, 1)
                for p in range(2):
                    b = it * 2 + p
                    pe.wait_ge(pT_ok, b + 1)
                    pe.wait_ge(v_ok, b + 1)
                    mm(bank[4 * p + 1][0:N, 0:D], prT[p], vs[p][:]).then_inc(pv_ps, 1)
                for p in range(2):
                    b = it * 2 + p
                    pe.wait_ge(h_ok, b + 1)
                    for k in range(DK):
                        last = turn(bank[4 * p][:, k * N:(k + 1) * N], hs[p][:, k * 128:(k + 1) * 128], ident[0:N, 0:N])
                    last.then_inc(hT_ps, 1)
                for p in range(2):
                    b = it * 2 + p
                    pe.wait_ge(hT_ok, b + 1)
                    for k in range(DK):
                        last = mm(bank[4 * p + 1][0:N, 0:D], xsT[p][:, k, :], wfc[:, k, :], start=(k == 0), stop=(k == DK - 1))
                    last.then_inc(fc_ps, 1)
                for p in range(2):
                    b = it * 2 + p
                    pe.wait_ge(x1_ok, b + 2)
                    for k in range(DK):
                        last = turn(bank[4 * p][:, k * N:(k + 1) * N], x1s[p][:, k * 128:(k + 1) * 128], ident[0:N, 0:N])
                    last.then_inc(x1T_ps, 1)
            pe.wait_ge(x1T_ok, B + 1)

            pe.wait_ge(cross_w, 16 * 11)
            pe.wait_ge(scaled, 9)

            def turn_context(b, u, p, k):
                if k == 0:
                    pe.wait_ge(c_in[p], 16 * (u + 1))
                for c in range(KC):
                    last = turn(bank[3][0:CK, c * KP:(c + 1) * KP], cx[p][:, c, k * CK:(k + 1) * CK], ident[0:KP, 0:KP])
                last.then_inc(cT_ps, 1)

            def values(b, u, p, chunks):
                for n, c in enumerate(chunks):
                    for k in range(2):
                        last = mm(bank[3][0:KP, n * D:(n + 1) * D], cxT[p][:, k, c * KP:(c + 1) * KP], xwv[:, k, :],
                                  start=(k == 0), stop=(k == 1))
                last.then_inc(vx_ps, 1)

            def queries(b, u, p):
                for m in range(DK):
                    for k in range(DK):
                        last = mm(bank[3][:, D + m * N:D + (m + 1) * N], xwq[:, k, m * 128:(m + 1) * 128],
                                  x1T[:, k, bass.ds(b * N, N)], start=(k == 0), stop=(k == DK - 1))
                last.then_inc(q_ps, 1)

            def keys(b, u, p, m):
                pe.wait_ge(cT_ok, 2 * (b + 1))
                for k in range(2):
                    last = mm(bank[3][:, 0:NK], xwk[:, k, m * 128:(m + 1) * 128], cxT[p][:, k, :], start=(k == 0), stop=(k == 1))
                last.then_inc(k_ps, 1)

            def mean_value(b, u, p):
                pe.wait_ge(oT_ok, b - 1)
                for n in range(DK):
                    for k in range(2):
                        last = mm(bank[6][:, 4 * N + n:4 * N + n + 1], xwv[:, k, n * 128:(n + 1) * 128], cxsum[p][:, k:k + 1],
                                  start=(k == 0), stop=(k == 1))
                last.then_inc(vm_ps, 1)

            def keys_gone(b, m):
                pe.wait_ge(k_rest, DK * b + m + 1)

            def scores(b, u, p, h):
                if h % (H // 2) == 0:
                    pe.wait_ge(stacked[h // (H // 2)][p], 16 * 6 * (u + 1))
                if h == 0:
                    pe.wait_ge(sx_max, H * b + 3)
                else:
                    pe.wait_ge(sx_max, H * b + h + 1)
                mm(bank[h % 3][0:N, 0:NK], qst[p][0:ROWS, h, :], kst[p][0:ROWS, h, :]).then_inc(sx_ps, 1)

            def scores_turned(b, u, p, g):
                if g == 0:
                    pe.wait_ge(mrow_in[p], 16 * (u + 1) + 16)
                pe.wait_ge(exp_ok, b * GROUPS + g + 1)
                i, c = g // KC, g % KC
                for j in range(4):
                    last = mm(bank[4 + g % 2][0:KP, j * N:(j + 1) * N], kst[p][0:ROWS + SHIFT, 4 * i + j, c * KP:(c + 1) * KP],
                              qst[p][0:ROWS + SHIFT, 4 * i + j, :])
                last.then_inc(st_ps, 1)

            def turn_maxima(b, u, p, first=False):
                pe.wait_ge(mparts_ok, b + 1)
                pe.wait_ge(floor_ok, b + 1)
                if not first:
                    pe.wait_ge(heads_ok, b - 1)
                pe.sem_inc(waits_met, 1)
                turn(bank[7][0:3 * H, 0:N // 2].bitcast(BF16), mparts[p][:].rearrange("q t h -> q (t h)"), identb[0:N, 0:N])
                turn(bank[7][0:H, 256:256 + N], floor[p][:], ident[0:N, 0:N]).then_inc(mT_ps, 1)

            def heads_of(b, u, p, i):
                pe.wait_ge(clip_ok, 4 * b + i + 1)
                if i == 0:
                    pe.wait_ge(oT_ok, b + 1)
                    pe.wait_ge(vm_ok, min(b + 3, B) if isinstance(b, int) else b + 3)
                for c in range(KC):
                    for j in range(4):
                        last = mm(bank[6][32 * j:32 * j + 32, i * N:(i + 1) * N], vx[p][:, c, 4 * i + j, :],
                                  prob[i][0:KP, c, j * N:(j + 1) * N], start=(c == 0), stop=(c == KC - 1))
                last.then_inc(prob_free, 1)

            def turn_heads(b, u, p, final=False):
                if not final:
                    pe.wait_ge(mT_ok, b + 2)
                pe.wait_ge(oT_ok, b + 2)
                for i in range(4):
                    last = turn(bank[7][0:N, i * 128:(i + 1) * 128], oT[p][:, i, :], ident[:, :])
                last.then_inc(o_ps, 1)

            def cross_step(it, s):
                static = isinstance(it, int)
                t = it * 2 + s
                one_on, two_on, three_on = (not static or s + n < B for n in (1, 2, 3))
                before, now, next_ = not static or s > 0, seq(it, s), seq(it, s + 1)
                if two_on:
                    pe.wait_ge(cT_ok, 2 * (t + 3))
                    keys(*seq(it, s + 2), 0)
                scores_turned(*now, 0)
                if one_on:
                    scores(*next_, 3)
                scores_turned(*now, 1)
                if before:
                    heads_of(t - 1, None, (s + 1) % 2, 3)
                if one_on:
                    scores(*next_, 4)
                scores_turned(*now, 2)
                if one_on:
                    if two_on:
                        keys_gone(t + 2, 0)
                    else:
                        pe.wait_ge(vx_ok, 2 * (t + 1))
                    values(*next_, (2,))
                    if two_on:
                        queries(*seq(it, s + 2))
                    scores(*next_, 5)
                    scores(*next_, 6)
                scores_turned(*now, 3)
                if before:
                    turn_heads(t - 1, None, (s + 1) % 2)
                if one_on:
                    scores(*next_, 7)
                scores_turned(*now, 4)
                if two_on:
                    pe.wait_ge(q_rest, t + 3)
                    keys(*seq(it, s + 2), 1)
                    mean_value(*seq(it, s + 2))
                if one_on:
                    scores(*next_, 8)
                    scores(*next_, 9)
                scores_turned(*now, 5)
                heads_of(*now, 0)
                if one_on:
                    scores(*next_, 10)
                scores_turned(*now, 6)
                if one_on:
                    pe.wait_ge(vx_ok, 2 * (t + 1) + 1)
                    if two_on:
                        keys_gone(t + 2, 1)
                    values(*next_, (0, 1))
                    scores(*next_, 11)
                    scores(*next_, 12)
                scores_turned(*now, 7)
                if one_on:
                    scores(*next_, 13)
                    scores(*next_, 14)
                scores_turned(*now, 8)
                if one_on:
                    scores(*next_, 15)
                heads_of(*now, 1)
                scores_turned(*now, 9)
                if three_on:
                    pe.wait_ge(vx_ok, 2 * (t + 2))
                    turn_context(*seq(it, s + 3), 0)
                if two_on:
                    scores(*seq(it, s + 2), 0)
                scores_turned(*now, 10)
                if one_on:
                    turn_maxima(*next_)
                if two_on:
                    scores(*seq(it, s + 2), 1)
                scores_turned(*now, 11)
                if two_on:
                    scores(*seq(it, s + 2), 2)
                heads_of(*now, 2)
                if three_on:
                    pe.wait_ge(cT_ok, 2 * (t + 3) + 1)
                    turn_context(*seq(it, s + 3), 1)

            for s in range(3):
                if s:
                    keys_gone(s - 1, 1)
                turn_context(*seq(0, s), 0)
                pe.wait_ge(cT_ok, 2 * s + 1)
                turn_context(*seq(0, s), 1)
                pe.wait_ge(cT_ok, 2 * s + 2)
                if s == 2:
                    break
                keys(*seq(0, s), 0)
                keys_gone(s, 0)
                if s == 0:
                    values(*seq(0, 0), (2,))
                queries(*seq(0, s))
                pe.wait_ge(vx_ok, 1)
                pe.wait_ge(q_rest, s + 1)
                keys(*seq(0, s), 1)
                if s:
                    pe.wait_ge(vm_ok, s)
                mean_value(1, None, s)
                if s == 0:
                    keys_gone(s, 1)
                    values(*seq(0, 0), (0, 1))
                    pe.wait_ge(vx_ok, 2)
            for h in range(H):
                scores(*seq(0, 0), h)
            turn_maxima(*seq(0, 0), first=True)
            for h in range(3):
                scores(*seq(0, 1), h)
            cross_step(0, 0)
            with pe.Fori(0, LOOPED // 2) as it:
                for s in range(1, 3):
                    cross_step(it, s)
            for s in range(LOOPED + 1, B):
                cross_step(0, s)
            heads_of(*seq(0, B - 1), 3)
            turn_heads(*seq(0, B - 1), final=True)
            pe.wait_ge(heads_ok, B)

            pe.wait_ge(nan_cnt, 1)
            mm(bank[0][:, 0:B * GROUPS], ones[:, :], flag[0:KP, 0:B * GROUPS]).then_inc(nan_ps, 1)
            pe.wait_ge(nan_ok, 1)

            with pe.Fori(0, B // 2) as it:
                for p in range(2):
                    b = it * 2 + p
                    pe.wait_ge(att_ok, b + 1)
                    pe.wait_ge(y_ok, 2 * it + 1)
                    for k in range(DK):
                        last = turn(bank[4 * p][:, k * N:(k + 1) * N], att[p][0:N, k * 128:(k + 1) * 128], ident[0:N, 0:N])
                    last.then_inc(aT_ps, 1)
                for p in range(2):
                    b = it * 2 + p
                    pe.wait_ge(aT_ok, b + 1)
                    for k in range(DK):
                        last = mm(bank[4 * p + 1][0:N, 0:D], attT[p][:, k, :], xwo[:, k, :], start=(k == 0), stop=(k == DK - 1))
                    last.then_inc(wo_ps, 1)
                for p in range(2):
                    b = it * 2 + p
                    pe.wait_ge(xq_ok, b + 1)
                    for k in range(DK):
                        last = turn(bank[4 * p][:, k * N:(k + 1) * N], xq[p][0:N, k * 128:(k + 1) * 128], ident[0:N, 0:N])
                    last.then_inc(xqT_ps, 1)
                for p in range(2):
                    b = it * 2 + p
                    pe.wait_ge(xqT_ok, b + 1)
                    for w, (W, s) in enumerate(((wgT, gate_ps), (wuT, up_ps))):
                        for u in range(2):
                            for k in range(DK):
                                last = mm(bank[4 * p + 2 * w + u][0:N, 0:FF // 2], xqT[p][:, k, :], W[:, k, u * FF // 2:(u + 1) * FF // 2],
                                          start=(k == 0), stop=(k == DK - 1))
                        last.then_inc(s, 1)
                for p in range(2):
                    b = it * 2 + p
                    pe.wait_ge(hq_ok, b + 1)
                    for c, (o, m) in enumerate(FT):
                        last = turn(bank[4 * p + c // 4][0:m, (c % 4) * N:(c % 4 + 1) * N], hq[p][0:N, o:o + m], ident[0:N, 0:N])
                    last.then_inc(hqT_ps, 1)
                for p in range(2):
                    b = it * 2 + p
                    pe.wait_ge(hqT_ok, b + 1)
                    for c, (o, m) in enumerate(FT):
                        last = mm(bank[4 * p + 2][0:N, 0:D], hqT[p][0:m, c, :], wdT[0:m, c, :], start=(c == 0), stop=(c == len(FT) - 1))
                    last.then_inc(dn_ps, 1)

        @block.scalar
        def _(act):
            def copy(o, i):
                return nc.scalar.copy(o, i)

            n = 0
            for w, WT in enumerate((wgT, wuT)):
                for k in range(DK):
                    for jh in range(2):
                        act.wait_ge(w_turned, n + 1)
                        copy(WT[:, k, jh * 352:(jh + 1) * 352], bank[n % 8][:, 0:352]).then_inc(w_kept, 1)
                        n += 1
            for c, (o, m) in enumerate(FT):
                act.wait_ge(w_turned, n + 1)
                copy(wdT[0:m, c, :], bank[n % 8][0:m, 0:D]).then_inc(w_kept, 1)
                n += 1

            with act.Fori(0, B // 2) as it:
                for p in range(2):
                    b = it * 2 + p
                    act.wait_ge(xT_ps, b + 1)
                    copy(xsT[p][:], bank[4 * p][:, 0:DK * N].rearrange("p (k n) -> p k n", n=N)).then_inc(xT_ok, 1)
                for p in range(2):
                    b = it * 2 + p
                    act.wait_ge(v_ps, b + 1)
                    copy(vs[p][:], bank[4 * p + 2][0:N, 0:D]).then_inc(v_ok, 1)
                for p in range(2):
                    b = it * 2 + p
                    act.wait_ge(s_max, b + 1)
                    nc.scalar.activation(pr[p], sc[p], ACT.Exp, bias=row[p][:, 0:1], accum_out=row[p][:, 1:2]).then_inc(p_ok, 1)
                for p in range(2):
                    b = it * 2 + p
                    act.wait_ge(pT_ps, b + 1)
                    copy(prT[p], bank[4 * p][0:N, 0:N]).then_inc(pT_ok, 1)
                for p in range(2):
                    b = it * 2 + p
                    act.wait_ge(hT_ps, b + 1)
                    copy(xsT[p][:], bank[4 * p][:, 0:DK * N].rearrange("p (k n) -> p k n", n=N)).then_inc(hT_ok, 1)
                for p in range(2):
                    b = it * 2 + p
                    act.wait_ge(x1T_ps, b + 1)
                    copy(x1T[:, :, bass.ds(b * N, N)], bank[4 * p][:, 0:DK * N].rearrange("p (k n) -> p k n", n=N)).then_inc(x1T_ok, 1)

            act.wait_ge(cross_w, 16 * 11)
            act.wait_ge(scaled, 9)

            def context_turned(b, u, p, k):
                act.wait_ge(cT_ps, 2 * b + k + 1)
                nc.scalar.activation(cxT[p][:, k, :], bank[3][0:CK, 0:NK], ACT.Identity, accum_out=cxsum[p][:, k:k + 1]).then_inc(cT_ok, 1)

            def queries_high(b, u, p, first=False):
                act.wait_ge(q_ps, b + 1)
                act.wait_ge(vx_ok, 1 if first else 2 * b - 1)
                for m in range(DK):
                    nc.scalar.activation(parts[p][:, 0, m, NK:NK + N], bank[3][:, D + m * N:D + (m + 1) * N], ACT.Identity,
                                         bias=bqT[:, m:m + 1]).then_inc(q_hi, 1)

            def keys_high(b, u, p, m, first=False):
                if m == 0 and not first:
                    for half in range(2):
                        act.wait_ge(to_dram[half][p], 32 * u)
                act.wait_ge(k_ps, DK * b + m + 1)
                nc.scalar.activation(parts[p][:, 0, m, 0:NK], bank[3][:, 0:NK], ACT.Identity, bias=bkT[:, m:m + 1]).then_inc(k_hi, 1)

            def mean_value(b, u, p):
                act.wait_ge(vm_ps, b + 1)
                for n in range(DK):
                    last = nc.scalar.activation(vmeanT[:, n, bass.ds(b, 1)], bank[6][:, 4 * N + n:4 * N + n + 1], ACT.Identity, bias=bvT[:, n:n + 1], scale=1.0 / NK)
                last.then_inc(vm_ok, 1)

            def floor_of(b, u, p):
                act.wait_ge(neg_ok, b + 1)
                nc.scalar.activation(floor[p][:], nmx[p][:, 0:H], ACT.Exp, bias=clampc[:, :]).then_inc(floor_ok, 1)

            def rows_of_maxima(b, u, p):
                act.wait_ge(mT_ps, b + 1)
                act.wait_ge(mrow_in[p], 16 * u + 16)
                act.wait_ge(floor_out[p], 16 * u + 16)
                copy(mrow[p][:], bank[7][0:3 * H, 0:N // 2].bitcast(BF16))
                copy(floorT[p][:], bank[7][0:H, 256:256 + N]).then_inc(mT_ok, 1)

            def weights(b, u, p, g):
                i, c = g // KC, g % KC
                if c == 0:
                    act.wait_ge(prob_free, 4 * b + i + 1)
                act.wait_ge(st_ps, b * GROUPS + g + 1)
                nc.scalar.activation(prob[i][0:KP, c, :], bank[4 + g % 2][0:KP, 0:4 * N], ACT.Exp,
                                     accum_out=wsum[:, bass.ds(b * GROUPS + g, 1)]).then_inc(exp_ok, 1)

            def heads_sum(b, u, p):
                act.wait_ge(prob_free, 4 * (b + 1) + 4)
                copy(oT[p][:], bank[6][:, 0:4 * N].rearrange("p (i n) -> p i n", n=N)).then_inc(oT_ok, 1)

            def cross_step(it, s):
                static = isinstance(it, int)
                one_on, two_on, three_on = (not static or s + n < B for n in (1, 2, 3))
                now = seq(it, s)
                if two_on:
                    keys_high(*seq(it, s + 2), 0)
                weights(*now, 0)
                weights(*now, 1)
                if not static or s > 0:
                    heads_sum(it * 2 + s - 1, None, (s + 1) % 2)
                weights(*now, 2)
                if two_on:
                    queries_high(*seq(it, s + 2))
                weights(*now, 3)
                weights(*now, 4)
                if two_on:
                    keys_high(*seq(it, s + 2), 1)
                    mean_value(*seq(it, s + 2))
                weights(*now, 5)
                weights(*now, 6)
                weights(*now, 7)
                weights(*now, 8)
                weights(*now, 9)
                if one_on:
                    floor_of(*seq(it, s + 1))
                if three_on:
                    context_turned(*seq(it, s + 3), 0)
                weights(*now, 10)
                if one_on:
                    rows_of_maxima(*seq(it, s + 1))
                weights(*now, 11)
                if three_on:
                    context_turned(*seq(it, s + 3), 1)

            for s in range(3):
                context_turned(*seq(0, s), 0)
                context_turned(*seq(0, s), 1)
                if s < 2:
                    keys_high(*seq(0, s), 0, first=True)
                    queries_high(*seq(0, s), first=True)
                    keys_high(*seq(0, s), 1, first=True)
                    mean_value(*seq(0, s))
            floor_of(*seq(0, 0))
            rows_of_maxima(*seq(0, 0))
            cross_step(0, 0)
            with act.Fori(0, LOOPED // 2) as it:
                for s in range(1, 3):
                    cross_step(it, s)
            for s in range(LOOPED + 1, B):
                cross_step(0, s)
            heads_sum(*seq(0, B - 1))

            with act.Fori(0, B // 2) as it:
                for p in range(2):
                    b = it * 2 + p
                    act.wait_ge(heads_ok, B)
                    act.wait_ge(nan_ok, 1)
                    act.wait_ge(aT_ps, 2 * it + 1)
                    copy(att[p][0:N], heads[:, b, :]).then_inc(att_ok, 1)
                for p in range(2):
                    b = it * 2 + p
                    act.wait_ge(aT_ps, b + 2)
                    copy(attT[p], bank[4 * p][:, 0:DK * N].rearrange("p (k n) -> p k n", n=N)).then_inc(aT_cp, 1)
                for p in range(2):
                    b = it * 2 + p
                    act.wait_ge(xqT_ps, b + 1)
                    copy(xqT[p], bank[4 * p][:, 0:DK * N].rearrange("p (k n) -> p k n", n=N)).then_inc(xqT_ok, 1)
                for p in range(2):
                    b = it * 2 + p
                    act.wait_ge(gate_ps, b + 1)
                    for u in range(2):
                        last = nc.scalar.activation(hat[p][0:N, u * FF // 2:(u + 1) * FF // 2], bank[4 * p + u][0:N, 0:FF // 2], ACT.Silu)
                    last.then_inc(silu_ok, 1)
                for p in range(2):
                    b = it * 2 + p
                    act.wait_ge(hqT_ps, b + 1)
                    copy(hqT[p][:, 0:4, :], bank[4 * p][:, 0:4 * N].rearrange("p (c n) -> p c n", n=N))
                    copy(hqT[p][:, 4, :], bank[4 * p + 1][:, 0:N])
                    copy(hqT[p][0:64, 5, :], bank[4 * p + 1][0:64, N:2 * N]).then_inc(hqT_ok, 1)

        @block.vector
        def _(dve):
            def quantise(steps, P, src, sc_, rs, t0, t1, dst):
                nb = src.free_size() // BLK
                blocks = lambda a: a.rearrange("p (b e) -> p b e", e=BLK)
                wide = lambda a: a.unsqueeze(2).broadcast_to([P, nb, BLK])
                v = nc.vector
                v.tensor_reduce(sc_, blocks(src), X, ALU.max, apply_absolute_value=True).then_inc(dve_step, 1)
                dve.wait_ge(dve_step, steps.next())
                v.tensor_scalar(sc_, sc_, 1.0 / 6.0, 1e-12, ALU.mult, ALU.max).then_inc(dve_step, 1)
                dve.wait_ge(dve_step, steps.next())
                v.reciprocal(rs, sc_).then_inc(dve_step, 1)
                dve.wait_ge(dve_step, steps.next())
                v.tensor_scalar(rs, rs, 1.0 - 2.0 ** -22, None, ALU.mult).then_inc(dve_step, 1)
                dve.wait_ge(dve_step, steps.next())
                v.tensor_scalar(t0.bitcast(U32), src.bitcast(U32), 0x7FFFFFFF, None, ALU.bitwise_and).then_inc(dve_step, 1)
                dve.wait_ge(dve_step, steps.next())
                v.tensor_tensor(blocks(t0), blocks(t0), wide(rs), ALU.mult).then_inc(dve_step, 1)
                dve.wait_ge(dve_step, steps.next())
                v.tensor_scalar(t1, t0, 1.0, HALF_UP, ALU.max, ALU.mult).then_inc(dve_step, 1)
                dve.wait_ge(dve_step, steps.next())
                v.tensor_tensor(t0, t0, t1, ALU.add).then_inc(dve_step, 1)
                dve.wait_ge(dve_step, steps.next())
                v.tensor_tensor(t0, t0, t1, ALU.subtract).then_inc(dve_step, 1)
                dve.wait_ge(dve_step, steps.next())
                v.tensor_tensor(blocks(t1), blocks(t0), wide(sc_), ALU.mult).then_inc(dve_step, 1)
                dve.wait_ge(dve_step, steps.next())
                return v.scalar_tensor_tensor(out=dst.bitcast(U32), in0=src.bitcast(U32), scalar=0x80000000, in1=t1.bitcast(U32),
                                              op0=ALU.bitwise_and, op1=ALU.bitwise_or)

            steps = Steps()
            dve.wait_ge(ffn_w, 48)
            for raw, P, L in ((raw_g, WP, WJ * D), (raw_u, WP, WJ * D), (raw_d, 128, 2 * FF)):
                flat = raw[0:P].rearrange("p j k -> p (j k)")
                s = scale[0][0:P, 0:L // BLK]
                r = scale[1][0:P, 0:L // BLK]
                quantise(steps, P, flat, s, r, tmp[0][0:P, 0:L], tmp[1][0:P, 0:L], flat).then_inc(w_quant, 1)
            dve.wait_ge(cross_w, 16 * 11)
            dve.wait_ge(consts, 1)
            for w, P, factor, raw in ((xwq, 128, HD ** -0.5, by_head[0]), (xwk, CK, 1.0, by_head[1])):
                for km in range(2 * DK):
                    columns = slice(km * 128, (km + 1) * 128)
                    nc.vector.tensor_scalar(w[:].rearrange("p k n -> p (k n)")[:, columns].rearrange("p (d h) -> p h d", d=HD),
                                            raw[0:P, columns].rearrange("p (h d) -> p h d", d=HD), factor, None, ALU.mult).then_inc(scaled, 1)
            nc.vector.tensor_scalar(bqT[:], bqT[:], HD ** -0.5, None, ALU.mult).then_inc(scaled, 1)
            dve.wait_ge(w_kept, 14)
            for p in range(2):
                last = nc.vector.memset(kst[p][ROWS:ROWS + SHIFT], 1.0)
            last.then_inc(w_kept, 1)

            def centre(steps, p, y, P):
                nc.vector.bn_stats(st6[p][0:P], y).then_inc(dve_step, 1)
                dve.wait_ge(dve_step, steps.next())
                dve.sem_inc(waits_met, 1)
                return nc.vector.bn_aggr(mv[p][0:P], st6[p][0:P])

            dve.wait_ge(self_w, 16 * 7)
            base = steps.n
            STEPS = 18
            with dve.Fori(0, B // 2) as it:
                steps = Steps(it * STEPS + base)
                for p in range(2):
                    b = it * 2 + p
                    dve.wait_ge(qk_ps, b + 1)
                    nc.vector.tensor_copy(qkT[p][:], bank[4 * p + 1][:, 0:4 * N].rearrange("p (k n) -> p k n", n=N)).then_inc(qk_ok, 1)
                for p in range(2):
                    b = it * 2 + p
                    dve.wait_ge(s_ps, b + 1)
                    nc.vector.scalar_tensor_tensor(out=sc[p], in0=bank[4 * p + 3][0:N, 0:N], scalar=D ** -0.5, in1=causal[:],
                                                           op0=ALU.mult, op1=ALU.add).then_inc(dve_step, 1)
                    dve.wait_ge(dve_step, steps.next())
                    nc.vector.tensor_reduce(row[p][:, 0:1], sc[p], X, ALU.max, negate=True).then_inc(s_max, 1)
                for p in range(2):
                    b = it * 2 + p
                    dve.wait_ge(p_ok, b + 1)
                    nc.vector.reciprocal(row[p][:, 2:3], row[p][:, 1:2]).then_inc(dve_step, 1)
                    dve.wait_ge(dve_step, steps.next())
                    dve.wait_ge(pv_ps, b + 1)
                    dve.wait_ge(v_ok, b + 1)
                    nc.vector.scalar_tensor_tensor(out=hs[p], in0=bank[4 * p + 1][0:N, 0:D], scalar=row[p][:, 2:3], in1=vs[p][:],
                                                           op0=ALU.mult, op1=ALU.add).then_inc(dve_step, 1)
                    dve.wait_ge(dve_step, steps.next())
                    centre(steps, p, hs[p], N).then_inc(var_ok, 1)
                for p in range(2):
                    b = it * 2 + p
                    dve.wait_ge(rstd_ok, 4 * it + p + 1)
                    nc.vector.tensor_scalar(hs[p], hs[p], mv[p][:, 0:1], rstd[p][:, 1:2], ALU.subtract, ALU.mult).then_inc(dve_step, 1)
                    dve.wait_ge(dve_step, steps.next())
                    nc.vector.tensor_tensor(hs[p], hs[p], gamma_b[:], ALU.mult).then_inc(dve_step, 1)
                    dve.wait_ge(dve_step, steps.next())
                    nc.vector.tensor_tensor(hs[p], hs[p], beta_b[:], ALU.add).then_inc(h_ok, 1)
                for p in range(2):
                    b = it * 2 + p
                    dve.wait_ge(fc_ps, b + 1)
                    nc.vector.tensor_tensor(x1s[p], bank[4 * p + 1][0:N, 0:D], xs[p][:], ALU.add).then_inc(dve_step, 1)
                    dve.wait_ge(dve_step, steps.next())
                    nc.vector.tensor_tensor(x1s[p], x1s[p], bfc_b[:], ALU.add).then_inc(dve_step, 1)
                    dve.wait_ge(dve_step, steps.next())
                    centre(steps, p, x1s[p], N).then_inc(var_ok, 1)
                for p in range(2):
                    b = it * 2 + p
                    dve.wait_ge(rstd_ok, 4 * it + 2 + p + 1)
                    nc.vector.tensor_scalar(x1[:, b, :], x1s[p], mv[p][:, 0:1], rstd[p][:, 1:2], ALU.subtract, ALU.mult)
                    nc.vector.tensor_scalar(x1s[p], x1s[p], mv[p][:, 0:1], rstd[p][:, 1:2], ALU.subtract, ALU.mult).then_inc(x1_ok, 1)
            assert steps.n == STEPS
            base += B // 2 * STEPS
            steps = Steps(base)

            def values(b, u, p, chunks, first=False, queries_of=None):
                if queries_of is None:
                    dve.wait_ge(vx_ps, 2 * b + (1 if chunks[0] else 2))
                else:
                    dve.wait_ge(q_ps, queries_of + 1)
                if not first and chunks[0]:
                    dve.wait_ge(prob_free, 4 * b)
                for n, c in enumerate(chunks):
                    last = nc.vector.tensor_tensor(vx[p][:, c, :, 0:HD], bank[3][0:KP, n * D:(n + 1) * D].rearrange("p (h d) -> p h d", d=HD),
                                                   bv_b[:].rearrange("p (h d) -> p h d", d=HD), ALU.add)
                last.then_inc(vx_ok, 1)

            def queries_rest(b, u, p):
                dve.wait_ge(q_hi, DK * (b + 1))
                for m in range(DK):
                    last = nc.vector.scalar_tensor_tensor(out=rest[p][:, m, NK:NK + N], in0=bank[3][:, D + m * N:D + (m + 1) * N], scalar=bqT[:, m:m + 1],
                                                          in1=parts[p][:, 0, m, NK:NK + N], op0=ALU.add, op1=ALU.subtract)
                last.then_inc(q_rest, 1)

            def keys_rest(b, u, p, m, first=False):
                if m == 0 and not first:
                    dve.wait_ge(split_ok, 4 * (b - 1))
                dve.wait_ge(k_hi, DK * b + m + 1)
                nc.vector.scalar_tensor_tensor(out=rest[p][:, m, 0:NK], in0=bank[3][:, 0:NK], scalar=bkT[:, m:m + 1],
                                               in1=parts[p][:, 0, m, 0:NK], op0=ALU.add, op1=ALU.subtract).then_inc(k_rest, 1)

            def maxima(b, u, p, *hs):
                for h in hs:
                    dve.wait_ge(sx_ps, H * b + h + 1)
                    nc.vector.tensor_reduce(nmx[p][:, H + h:H + h + 1], bank[h % 3][0:N, 0:NK], X, ALU.max, negate=True).then_inc(sx_max, 1)

            def shifts(b, u, p):
                dve.wait_ge(sx_max, H * (b + 1) + 3)
                nc.vector.tensor_scalar(nmx[p][:, 0:H], nmx[p][:, H:2 * H], CLAMP, -CLAMP, ALU.min, ALU.max).then_inc(neg_ok, 1)
                dve.wait_ge(neg_ok, b + 1)
                nc.vector.tensor_copy(mparts[p][:, 0, :], nmx[p][:, 0:H]).then_inc(dve_step, 1)
                dve.wait_ge(dve_step, steps.next())
                nc.vector.tensor_tensor(nmx[p][:, H:2 * H], nmx[p][:, 0:H], mparts[p][:, 0, :], ALU.subtract).then_inc(dve_step, 1)
                dve.wait_ge(dve_step, steps.next())
                nc.vector.tensor_copy(mparts[p][:, 1, :], nmx[p][:, H:2 * H]).then_inc(dve_step, 1)
                dve.wait_ge(dve_step, steps.next())
                nc.vector.tensor_tensor(mparts[p][:, 2, :], nmx[p][:, H:2 * H], mparts[p][:, 1, :], ALU.subtract).then_inc(mparts_ok, 1)

            def clip(b, u, p, i):
                if i == 0:
                    dve.wait_ge(floor_in[p], 16 * (u + 1))
                dve.wait_ge(exp_ok, b * GROUPS + KC * (i + 1) + 2)
                fl = floor_b[:, 4 * i * N:4 * (i + 1) * N].unsqueeze(1).broadcast_to([KP, KC, 4 * N])
                nc.vector.scalar_tensor_tensor(out=prob[i][0:KP], in0=prob[i][0:KP], scalar=1.0, in1=fl, op0=ALU.min, op1=ALU.max).then_inc(clip_ok, 1)

            def heads_out(b, u, p):
                dve.wait_ge(o_ps, b + 1)
                o4 = bank[7][0:N, :].rearrange("q (h e) -> q h e", e=32)
                nc.vector.reciprocal(rden[p][:], o4[:, :, HD]).then_inc(dve_step, 1)
                dve.wait_ge(dve_step, steps.next())
                nc.vector.tensor_tensor(heads[:, bass.ds(b, 1), :].rearrange("q b (h d) -> q (b h) d", d=HD), o4[:, :, 0:HD],
                                        rden[p][:].unsqueeze(2).broadcast_to([N, H, HD]), ALU.mult).then_inc(heads_ok, 1)

            def cross_step(it, s):
                static = isinstance(it, int)
                one_on, two_on = (not static or s + n < B for n in (1, 2))
                before = not static or s > 0
                now, next_, previous = seq(it, s), seq(it, s + 1), (it * 2 + s - 1, None, (s + 1) % 2)
                if before:
                    clip(*previous, 3)
                if two_on:
                    keys_rest(*seq(it, s + 2), 0)
                if one_on:
                    maxima(*next_, 3)
                if one_on:
                    maxima(*next_, 4)
                    values(*next_, (2,), queries_of=it * 2 + s + 2 if two_on else None)
                    maxima(*next_, 5)
                if two_on:
                    queries_rest(*seq(it, s + 2))
                if one_on:
                    maxima(*next_, 6)
                clip(*now, 0)
                if one_on:
                    maxima(*next_, 7)
                if before:
                    heads_out(*previous)
                if two_on:
                    keys_rest(*seq(it, s + 2), 1)
                if one_on:
                    maxima(*next_, 8, 9, 10)
                clip(*now, 1)
                if one_on:
                    values(*next_, (0, 1))
                    maxima(*next_, 11, 12, 13, 14, 15)
                    shifts(*next_)
                clip(*now, 2)
                if two_on:
                    maxima(*seq(it, s + 2), 0, 1, 2)

            for s in range(2):
                keys_rest(*seq(0, s), 0, first=True)
                if s == 0:
                    values(*seq(0, 0), (2,), first=True, queries_of=0)
                queries_rest(*seq(0, s))
                keys_rest(*seq(0, s), 1)
                if s == 0:
                    values(*seq(0, 0), (0, 1), first=True)
            maxima(*seq(0, 0), *range(H))
            shifts(*seq(0, 0))
            maxima(*seq(0, 1), 0, 1, 2)
            cross_step(0, 0)
            base = steps.base + steps.n
            CS = 8
            with dve.Fori(0, LOOPED // 2) as it:
                steps = Steps(it * CS + base)
                for s in range(1, 3):
                    cross_step(it, s)
            assert steps.n == CS
            steps = Steps(base + LOOPED // 2 * CS)
            for s in range(LOOPED + 1, B):
                cross_step(0, s)
            clip(*seq(0, B - 1), 3)
            heads_out(*seq(0, B - 1))
            base = steps.base + steps.n
            steps = Steps(base)
            dve.wait_ge(exp_ok, B * GROUPS + 2)
            nc.vector.tensor_tensor(flag[0:KP, 0:B * GROUPS], wsum[:, :], wsum[:, :], ALU.not_equal).then_inc(nan_cnt, 1)
            dve.wait_ge(nan_ps, 1)
            nc.vector.tensor_reduce(flag[:, B * GROUPS:B * GROUPS + 1], bank[0][:, 0:B * GROUPS], X, ALU.max).then_inc(dve_step, 1)
            dve.wait_ge(dve_step, steps.next())
            nc.vector.tensor_scalar(nanmask[:, :], flag[:, B * GROUPS:B * GROUPS + 1], 0.0, None, ALU.is_gt).then_inc(nan_ok, 1)
            dve.wait_ge(nan_ok, 1)
            base = steps.base + steps.n
            FS = 58
            with dve.Fori(0, B // 2) as it:
                steps = Steps(it * FS + base)
                for p in range(2):
                    b = it * 2 + p
                    dve.wait_ge(aT_cp, b + 1)
                    nc.vector.tensor_copy(vmean[p][:, :, :], vmeanT[:, :, bass.ds(b, 1)]).then_inc(dve_step, 1)
                    dve.wait_ge(dve_step, steps.next())
                    dve.sem_inc(waits_met, 1)
                    for k in range(DK):
                        last = nc.vector.copy_predicated(attT[p][:, k, :], nanmask[:, 0:1].broadcast_to([128, N]),
                                                         vmean[p][:, k, :].broadcast_to([128, N]))
                    last.then_inc(aT_ok, 1)
                for p in range(2):
                    b = it * 2 + p
                    dve.wait_ge(wo_ps, b + 1)
                    nc.vector.tensor_tensor(x2[p][0:N], bank[4 * p + 1][0:N, 0:D], bo_b[:], ALU.add).then_inc(dve_step, 1)
                    dve.wait_ge(dve_step, steps.next())
                    nc.vector.tensor_tensor(x2[p][0:N], x2[p][0:N], x1[:, b, :], ALU.add).then_inc(dve_step, 1)
                    dve.wait_ge(dve_step, steps.next())
                    centre(steps, p, x2[p][0:N], N).then_inc(varf, 1)
                for p in range(2):
                    b = it * 2 + p
                    dve.wait_ge(rstdf, 4 * it + p + 1)
                    nc.vector.tensor_scalar(x2[p][0:N], x2[p][0:N], mv[p][:, 0:1], rstd[p][:, 1:2], ALU.subtract, ALU.mult).then_inc(dve_step, 1)
                    dve.wait_ge(dve_step, steps.next())
                    nb = D // BLK
                    quantise(steps, N, x2[p][0:N], scale[p][0:N, 0:nb], scale[p][0:N, 128:128 + nb], ft[p][0][0:N, 0:D], ft[p][1][0:N, 0:D],
                             xq[p][0:N]).then_inc(xq_ok, 1)
                for p in range(2):
                    b = it * 2 + p
                    dve.wait_ge(silu_ok, b + 1)
                    dve.wait_ge(up_ps, b + 1)
                    for u in range(2):
                        half = hat[p][0:N, u * FF // 2:(u + 1) * FF // 2]
                        nc.vector.tensor_tensor(half, half, bank[4 * p + 2 + u][0:N, 0:FF // 2], ALU.mult).then_inc(dve_step, 1)
                        dve.wait_ge(dve_step, steps.next())
                    nb = FF // BLK
                    quantise(steps, N, hat[p][0:N], scale[p][0:N, 0:nb], scale[p][0:N, 128:128 + nb], ft[p][0][0:N], ft[p][1][0:N],
                             hq[p][0:N]).then_inc(hq_ok, 1)
                for p in range(2):
                    b = it * 2 + p
                    dve.wait_ge(dn_ps, b + 1)
                    dve.wait_ge(y_out[p], 16 * it + 16)
                    nc.vector.tensor_tensor(yo[p][0:N], bank[4 * p + 2][0:N, 0:D], x2[p][0:N], ALU.add).then_inc(dve_step, 1)
                    dve.wait_ge(dve_step, steps.next())
                    centre(steps, p, yo[p][0:N], N).then_inc(varf, 1)
                for p in range(2):
                    b = it * 2 + p
                    dve.wait_ge(rstdf, 4 * it + 2 + p + 1)
                    nc.vector.tensor_scalar(yo[p][0:N], yo[p][0:N], mv[p][:, 0:1], rstd[p][:, 1:2], ALU.subtract, ALU.mult).then_inc(y_ok, 1)
            assert steps.n == FS

        @block.gpsimd
        def _(pool):
            for free, credit in credited:
                pool.sem_inc(free, credit)
            steps = Steps()
            for t in (ident, identb, causal):
                nc.gpsimd.memset(t[:], 0.0).then_inc(pool_step, 1)
                pool.wait_ge(pool_step, steps.next())
            for t in (ident, identb):
                nc.gpsimd.affine_select(out=t[:], in_=t[:], compare_op=ALU.not_equal, fill=1.0, base=0, pattern=[[-1, 128]], channel_multiplier=1).then_inc(pool_step, 1)
                pool.wait_ge(pool_step, steps.next())
            nc.gpsimd.affine_select(out=causal[:], in_=causal[:], compare_op=ALU.is_ge, fill=-3e38, base=0, pattern=[[-1, N]], channel_multiplier=1).then_inc(pool_step, 1)
            pool.wait_ge(pool_step, steps.next())
            nc.gpsimd.memset(mhalf[:], -0.5).then_inc(pool_step, 1)
            pool.wait_ge(pool_step, steps.next())
            nc.gpsimd.memset(clampc[:], -CLAMP).then_inc(pool_step, 1)
            pool.wait_ge(pool_step, steps.next())
            nc.gpsimd.memset(ones[:], 1.0).then_inc(pool_step, 1)
            pool.wait_ge(pool_step, steps.next())
            for p in range(2):
                nc.gpsimd.memset(vx[p][:], 0.0).then_inc(pool_step, 1)
                pool.wait_ge(pool_step, steps.next())
                nc.gpsimd.memset(vx[p][:, :, :, HD:HD + 1], 1.0).then_inc(pool_step, 1)
                pool.wait_ge(pool_step, steps.next())
            nc.gpsimd.memset(flag[:, B * GROUPS:], 0.0).then_inc(consts, 1)
            base = steps.n

            def root(steps, p):
                pool.sem_inc(waits_met, 1)
                nc.gpsimd.tensor_scalar(rstd[p][:, 0:1], mv[p][:, 1:2], EPS, None, ALU.add).then_inc(pool_step, 1)
                pool.wait_ge(pool_step, steps.next())
                return nc.gpsimd.tensor_tensor(rstd[p][:, 1:2], rstd[p][:, 0:1], mhalf[0:N, :], ALU.pow)

            with pool.Fori(0, B // 2) as it:
                steps = Steps(it * 4 + base)
                for r in range(2):
                    for p in range(2):
                        pool.wait_ge(var_ok, 4 * it + 2 * r + p + 1)
                        root(steps, p).then_inc(rstd_ok, 1)
            base += B // 2 * 4
            steps = Steps(base)

            def split(b, u, p, first=False):
                if not first:
                    for half in range(2):
                        pool.wait_ge(to_dram[half][p], 32 * u)
                        pool.sem_inc(waits_met, 1)
                for lo, hi, m in ((0, NK, 0), (NK, NK + N, 0), (NK, NK + N, 1), (0, NK, 1)):
                    if lo:
                        pool.wait_ge(q_rest, b + 1)
                    else:
                        pool.wait_ge(k_rest, DK * b + m + 1)
                    pool.sem_inc(waits_met, 1)
                    nc.gpsimd.tensor_copy(parts[p][:, 1, m, lo:hi], rest[p][:, m, lo:hi]).then_inc(pool_step, 1)
                    pool.wait_ge(pool_step, steps.next())
                    nc.gpsimd.tensor_tensor(parts[p][:, 2, m, lo:hi], rest[p][:, m, lo:hi], parts[p][:, 1, m, lo:hi], ALU.subtract).then_inc(split_ok, 1)

            split(*seq(0, 0), first=True)
            split(*seq(0, 1), first=True)
            base = steps.base + steps.n
            with pool.Fori(0, B // 2 - 1) as it:
                steps = Steps(it * 8 + base)
                for s in range(2, 4):
                    split(*seq(it, s))
            assert steps.n == 8
            base += (B // 2 - 1) * 8
            with pool.Fori(0, B // 2) as it:
                steps = Steps(it * 4 + base)
                for r in range(2):
                    for p in range(2):
                        pool.wait_ge(varf, 4 * it + 2 * r + p + 1)
                        root(steps, p).then_inc(rstdf, 1)


_INS = ['x', 'ctx_768', 'L0_attn_Wq', 'L0_attn_Wk', 'L0_attn_Wv', 'L0_attn_Wfc', 'L0_attn_bfc', 'L0_attn_gamma', 'L0_attn_beta',
        'L0_xattn_Wq', 'L0_xattn_bq', 'L0_xattn_Wk', 'L0_xattn_bk', 'L0_xattn_Wv', 'L0_xattn_bv', 'L0_xattn_Wo', 'L0_xattn_bo',
        'L0_ffn_w_gate', 'L0_ffn_w_up', 'L0_ffn_w_down']
_OUTS = [((16, 112, 256), 'float32')]


def kernel(**inputs):
    import numpy as _np
    import concourse.bacc as _bacc
    from concourse import mybir as _mybir
    from concourse.bass_utils import run_bass_kernel_spmd as _run

    nc = _bacc.Bacc("TRN2", target_bir_lowering=False, num_devices=1)
    arrays, args = {}, []
    for name in _INS:
        a = _np.ascontiguousarray(inputs[name])
        arrays[f"in_{name}_dram"] = a
        args.append(nc.dram_tensor(f"in_{name}_dram", a.shape, _mybir.dt.from_np(a.dtype), kind="ExternalInput").ap())
    for i, (shape, dtype) in enumerate(_OUTS):
        dt = _mybir.dt.from_np(_np.dtype(dtype))
        args.append(nc.dram_tensor(f"out_{i}_dram", shape, dt, kind="ExternalOutput").ap())
    decoder_layer(nc, *args)
    r = _run(nc, [arrays], core_ids=[0])
    got = tuple(r.results[0][f"out_{i}_dram"] for i in range(len(_OUTS)))
    return got[0]
```
